# Optimizing a Trainium2 kernel written in Bass

```python
import numpy as np
import jax
import jax.numpy as jnp

def _softmax(x, axis=-1):
    return jax.nn.softmax(x, axis=axis)

def _gelu(x):
    return jax.nn.gelu(x, approximate=True)

def _silu(x):
    return jax.nn.silu(x)

def _sigmoid(x):
    return jax.nn.sigmoid(x)

def _layernorm(x, axis=-1, eps=1e-05):
    m = jnp.mean(x, axis=axis, keepdims=True)
    v = jnp.var(x, axis=axis, keepdims=True)
    return (x - m) / jnp.sqrt(v + eps)

def _scatter_add(tgt, idx, src, axis=0):
    return tgt.at[idx].add(src)

def _segment_sum(src, seg, n):
    return jax.ops.segment_sum(src, seg, n)
kernel_name = 'mk_decoder_postln_d1_seqx_r4_97d4a1'

def setup_inputs(seed: int=0):
    np.random.seed(seed)
    _w = jnp.asarray

    def _rec_inputs():
        import jax
        import jax.numpy as jnp
        _rk = jax.random.key(seed)
        x = -0.0003929 + 0.9999 * jax.random.normal(jax.random.fold_in(_rk, 1), (32, 128, 1024), jnp.float32)
        _lenS = 128 - jax.random.randint(jax.random.fold_in(_rk, 7), (32,), 0, max(1, 128 // 4) + 1, jnp.int32)
        _lenS2 = 128 - jax.random.randint(jax.random.fold_in(_rk, 8), (32,), 0, max(1, 128 // 4) + 1, jnp.int32)
        _ctx_4096P = jax.random.normal(jax.random.fold_in(_rk, 11), (32, 16, 1024), jnp.float32)
        _ctx_4096c = jax.random.dirichlet(jax.random.fold_in(_rk, 511), 0.3 * jnp.ones((16,), jnp.float32), (32, 128))
        _ctx_4096t = jnp.einsum('bsk,bkd->bsd', _ctx_4096c, _ctx_4096P)
        _ctx_4096t = _ctx_4096t * jax.lax.rsqrt(jnp.mean(jnp.square(_ctx_4096t)) + 1e-12) * 0.953939
        ctx_4096 = 2.81802e-05 + 1.00001 * (_ctx_4096t + 0.3 * jax.random.normal(jax.random.fold_in(_rk, 611), (32, 128, 1024), jnp.float32))
        return (x, ctx_4096)
    x, ctx_4096 = _rec_inputs()

    def _L0_attn_setup():
        import jax, jax.numpy as jnp
        import numpy as np
        import math
        HIDDEN = 1024
        N_HEADS = 32
        N_KV_HEADS = 8
        HEAD_DIM = HIDDEN // N_HEADS
        GROUPS = N_HEADS // N_KV_HEADS
        ROPE_THETA = 10000.0
        TOKEN_BUDGET = 128
        INIT_BUDGET = 128
        RECENT_BUDGET = 128
        CHUNK = 16
        B, S = (1, 512)

        def _rotate_half(x):
            x1, x2 = jnp.split(x, 2, axis=-1)
            return jnp.concatenate([-x2, x1], axis=-1)

        def _rope(seq_len, dtype):
            inv_freq = 1.0 / ROPE_THETA ** (jnp.arange(0, HEAD_DIM, 2, dtype=jnp.float32) / HEAD_DIM)
            freqs = jnp.arange(seq_len, dtype=jnp.float32)[:, None] * inv_freq[None, :]
            emb = jnp.concatenate([freqs, freqs], axis=-1)
            return (jnp.cos(emb).astype(dtype), jnp.sin(emb).astype(dtype))
        key = jax.random.key(seed)
        ks = jax.random.split(key, 5)
        sc = 0.02
        return {'hidden_states': jax.random.normal(ks[0], (B, S, HIDDEN), dtype=jnp.float32), 'wq': jax.random.normal(ks[1], (N_HEADS * HEAD_DIM, HIDDEN), dtype=jnp.float32) * sc, 'wk': jax.random.normal(ks[2], (N_KV_HEADS * HEAD_DIM, HIDDEN), dtype=jnp.float32) * sc, 'wv': jax.random.normal(ks[3], (N_KV_HEADS * HEAD_DIM, HIDDEN), dtype=jnp.float32) * sc, 'wo': jax.random.normal(ks[4], (HIDDEN, N_HEADS * HEAD_DIM), dtype=jnp.float32) * sc}
    _L0_attn_all = _L0_attn_setup()
    _L0_attn_in = {k: v for k, v in _L0_attn_all.items() if k in ('wq', 'wk', 'wv', 'wo')}
    del _L0_attn_all

    def _L0_xattn_setup():
        import jax, jax.numpy as jnp
        import numpy as np
        EPS = 1e-08

        def _cosine_sim(a, b):
            na = jnp.maximum(jnp.sqrt(jnp.sum(a * a, axis=1)), EPS)
            nb = jnp.maximum(jnp.sqrt(jnp.sum(b * b, axis=1)), EPS)
            return jnp.sum(a * b, axis=1) / (na * nb)
        key = jax.random.key(seed)
        k1, k2, k3 = jax.random.split(key, 3)
        B, C, T, O, K = (8, 128, 1024, 128, 3)
        feature = jax.random.normal(k1, (B, C, T), dtype=jnp.float32)
        embedding = jax.random.normal(k2, (B, C, T), dtype=jnp.float32)
        weight = jax.random.normal(k3, (O, C, K), dtype=jnp.float32) * 0.05
        return {'feature': feature, 'embedding': embedding, 'weight': weight}
    _L0_xattn_all = _L0_xattn_setup()
    _L0_xattn_in = {k: v for k, v in _L0_xattn_all.items() if k in ('weight',)}
    del _L0_xattn_all

    def _L0_ffn_setup():
        import jax, jax.numpy as jnp
        import numpy as np
        ALPHA = 32
        R = 16
        SCALING = ALPHA / R
        key = jax.random.key(seed)
        k1, k2, k3, k4 = jax.random.split(key, 4)
        B_, S, D = (4, 512, 1024)
        H, r, O = (8, R, 1024)
        x = jax.random.normal(k1, (B_, S, D), dtype=jnp.float32)
        A = jax.random.normal(k2, (H, r, D), dtype=jnp.float32) * 0.02
        Bm = jax.random.normal(k3, (H, O, r), dtype=jnp.float32) * 0.02
        Wr = jax.random.normal(k4, (H, D), dtype=jnp.float32) * 0.02
        br = jnp.zeros((H,), dtype=jnp.float32)
        return {'x': x, 'A': A, 'B': Bm, 'Wr': Wr, 'br': br}
    _L0_ffn_all = _L0_ffn_setup()
    _L0_ffn_in = {k: v for k, v in _L0_ffn_all.items() if k in ('A', 'B', 'Wr', 'br')}
    del _L0_ffn_all
    return {'x': x, 'ctx_4096': ctx_4096, 'L0_attn_wq': _L0_attn_in['wq'], 'L0_attn_wk': _L0_attn_in['wk'], 'L0_attn_wv': _L0_attn_in['wv'], 'L0_attn_wo': _L0_attn_in['wo'], 'L0_xattn_weight': _L0_xattn_in['weight'], 'L0_ffn_A': _L0_ffn_in['A'], 'L0_ffn_B': _L0_ffn_in['B'], 'L0_ffn_Wr': _L0_ffn_in['Wr'], 'L0_ffn_br': _L0_ffn_in['br']}

def reference(x, ctx_4096, L0_attn_wq, L0_attn_wk, L0_attn_wv, L0_attn_wo, L0_xattn_weight, L0_ffn_A, L0_ffn_B, L0_ffn_Wr, L0_ffn_br):
    import jax
    import jax.numpy as jnp

    def _L0_attn_ref(hidden_states, wq, wk, wv, wo):
        import jax, jax.numpy as jnp
        import numpy as np
        import math
        HIDDEN = 1024
        N_HEADS = 32
        N_KV_HEADS = 8
        HEAD_DIM = HIDDEN // N_HEADS
        GROUPS = N_HEADS // N_KV_HEADS
        ROPE_THETA = 10000.0
        TOKEN_BUDGET = 128
        INIT_BUDGET = 128
        RECENT_BUDGET = 128
        CHUNK = 16
        B, S = (1, 512)

        def _rotate_half(x):
            x1, x2 = jnp.split(x, 2, axis=-1)
            return jnp.concatenate([-x2, x1], axis=-1)

        def _rope(seq_len, dtype):
            inv_freq = 1.0 / ROPE_THETA ** (jnp.arange(0, HEAD_DIM, 2, dtype=jnp.float32) / HEAD_DIM)
            freqs = jnp.arange(seq_len, dtype=jnp.float32)[:, None] * inv_freq[None, :]
            emb = jnp.concatenate([freqs, freqs], axis=-1)
            return (jnp.cos(emb).astype(dtype), jnp.sin(emb).astype(dtype))
        b, s, _ = hidden_states.shape
        dtype = hidden_states.dtype
        NEG = jnp.finfo(dtype).min
        q = (hidden_states @ wq.T).reshape(b, s, N_HEADS, HEAD_DIM).transpose(0, 2, 1, 3)
        k = (hidden_states @ wk.T).reshape(b, s, N_KV_HEADS, HEAD_DIM).transpose(0, 2, 1, 3)
        v = (hidden_states @ wv.T).reshape(b, s, N_KV_HEADS, HEAD_DIM).transpose(0, 2, 1, 3)
        cos, sin = _rope(s, dtype)
        q = q * cos[None, None] + _rotate_half(q) * sin[None, None]
        k = k * cos[None, None] + _rotate_half(k) * sin[None, None]
        k = jnp.repeat(k, GROUPS, axis=1)
        v = jnp.repeat(v, GROUPS, axis=1)
        scores = jnp.einsum('bhqd,bhkd->bhqk', q, k) / math.sqrt(HEAD_DIM)
        q_pos = jnp.arange(s)[:, None]
        k_pos = jnp.arange(s)[None, :]
        causal = k_pos <= q_pos
        masked = jnp.where(causal[None, None], scores, NEG)
        pad = -s % CHUNK
        padded = jnp.pad(masked, ((0, 0), (0, 0), (0, 0), (0, pad)), constant_values=NEG)
        n_chunks = (s + pad) // CHUNK
        chunk_max = padded.reshape(b, N_HEADS, s, n_chunks, CHUNK).max(axis=-1)
        k_top = min(max(3, TOKEN_BUDGET // CHUNK), n_chunks)
        _, topk_idx = jax.lax.top_k(chunk_max, k_top)
        chunk_mask = jnp.any(topk_idx[..., None] == jnp.arange(n_chunks), axis=-2)
        tok_mask = jnp.repeat(chunk_mask, CHUNK, axis=-1)[..., :s]
        init_mask = k_pos < INIT_BUDGET
        recent_mask = k_pos > q_pos - RECENT_BUDGET
        allowed = causal[None, None] & (tok_mask | init_mask[None, None] | recent_mask[None, None])
        final = jnp.where(allowed, scores, NEG)
        attn = jax.nn.softmax(final, axis=-1)
        out = jnp.einsum('bhqk,bhkd->bhqd', attn, v)
        out = out.transpose(0, 2, 1, 3).reshape(b, s, N_HEADS * HEAD_DIM)
        return out @ wo.T

    def _L0_xattn_ref(feature, embedding, weight):
        import jax, jax.numpy as jnp
        import numpy as np
        EPS = 1e-08

        def _cosine_sim(a, b):
            na = jnp.maximum(jnp.sqrt(jnp.sum(a * a, axis=1)), EPS)
            nb = jnp.maximum(jnp.sqrt(jnp.sum(b * b, axis=1)), EPS)
            return jnp.sum(a * b, axis=1) / (na * nb)
        B, C, T = feature.shape
        O = weight.shape[0]
        K = 3
        emb_l = jnp.pad(embedding[:, :, :-1], ((0, 0), (0, 0), (1, 0)))
        emb_r = jnp.pad(embedding[:, :, 1:], ((0, 0), (0, 0), (0, 1)))
        sim = jnp.stack([_cosine_sim(embedding, emb_l), _cosine_sim(embedding, embedding), _cosine_sim(embedding, emb_r)], axis=1)
        att = jnp.repeat(sim, C, axis=1)
        f_pad = jnp.pad(feature, ((0, 0), (0, 0), (1, 1)))
        inp_unf = jnp.stack([f_pad[:, :, k:k + T] for k in range(K)], axis=2)
        inp_unf = inp_unf.reshape(B, C * K, T)
        w_flat = weight.reshape(O, C * K)
        out = jnp.einsum('bit,oi->bot', inp_unf * att, w_flat)
        return out

    def _L0_ffn_ref(x, A, B, Wr, br):
        import jax, jax.numpy as jnp
        import numpy as np
        ALPHA = 32
        R = 16
        SCALING = ALPHA / R
        H = A.shape[0]
        router_logits = jnp.einsum('bsd,hd->bsh', x, Wr) + br
        scores = H * jax.nn.softmax(router_logits, axis=-1)
        low = jnp.einsum('bsd,hrd->bshr', x, A)
        out = jnp.einsum('bshr,hor,bsh->bso', low, B, scores)
        return SCALING * out
    x = _layernorm(x + _L0_attn_ref(x, L0_attn_wq, L0_attn_wk, L0_attn_wv, L0_attn_wo), axis=-1)
    x = _layernorm(x + _L0_xattn_ref(x, ctx_4096, L0_xattn_weight), axis=-1)
    x = _layernorm(x + _L0_ffn_ref(x, L0_ffn_A, L0_ffn_B, L0_ffn_Wr, L0_ffn_br), axis=-1)
    return x

_drawn_inputs = setup_inputs


def setup_inputs(seed=0):
    import zlib

    import numpy as np

    out = dict(_drawn_inputs(seed))
    spreads = {'L0_ffn_br': (0.0, 0.1)}
    factors = {}
    for name, (base, spread) in spreads.items():
        noise = np.random.default_rng([zlib.crc32(name.encode()), seed]).standard_normal(out[name].shape)
        drawn = base * np.exp(spread * noise) if base else spread * noise
        out[name] = jnp.asarray(drawn.astype(out[name].dtype))
    for name, factor in factors.items():
        out[name] = (out[name] * factor).astype(out[name].dtype)
    return out
```

```python
from contextlib import ExitStack

import numpy as np

import concourse.bass as bass
from concourse import mybir

F32 = mybir.dt.float32
F32R = mybir.dt.float32r
ALU = mybir.AluOpType
ACT = mybir.ActivationFunctionType
AX = mybir.AxisListType

B, S, D = 32, 128, 1024
P = 128
KT = D // P
HEADS, KVH, DH = 32, 8, 32
NU = 2
NI = KVH // NU
NJ = HEADS // KVH
NC = NU * NJ
HALF = DH // 2
BANK = 512
KV = KVH * DH
NG = 3
SLOTS = NG * KT
R, H = 16, 8
HR = H * R
LOWW = HR + H
FFN_SCALE = float(H) * 2.0
LN_EPS = 1e-5
COS_EPS = 1e-8
MASKED = 1e30
TAPS = 3


def after(t, per, k):
    return t * per + k


def arrivals(t, par):
    return (t - par) * (16 // 2) + 16


def wait(eng, sem, count):
    if isinstance(count, int) and count <= 0:
        return
    eng.wait_ge(sem, count)


def valid(t):
    return not isinstance(t, int) or 0 <= t < B


def steps(eng, step, first, last, lead, tail):
    lo, hi = first + lead, last - tail + 1
    assert lo % 2 == 0 and hi % 2 == 0
    for t in range(first, lo):
        step(t, t % 2)
    with eng.Fori(lo // 2, hi // 2) as i:
        step(i * 2, 0)
        step(i * 2 + 1, 1)
    for t in range(hi, last + 1):
        step(t, t % 2)


def build(nc, xT, x, ctx_in, wqkv, wo, wx, wa, wb, br, rope, mask, ident, tapsel, out):
    ot_dram = nc.dram_tensor("ot_scratch", [B, P, D], F32, kind="Internal").ap()
    cs_dram = nc.dram_tensor("cs_scratch", [B, 4, BANK], F32, kind="Internal").ap()
    sim_dram = nc.dram_tensor("sim_scratch", [B, 2 * TAPS, D], F32, kind="Internal").ap()
    with ExitStack() as both:
        weights = both.enter_context(nc.sbuf_tensor("weights", [P, 2 * NG * KT * BANK], F32R))
        with ExitStack() as ctx:
            part1(nc, ctx, weights, xT, ctx_in, wqkv, rope, mask, ident, ot_dram, cs_dram)
        with ExitStack() as ctx:
            part2(nc, ctx, weights, x, wo, wx, wa, wb, br, ident, tapsel, ot_dram, cs_dram,
                  sim_dram, out)


def part1(nc, ctx, weights, xT, ctx_in, wqkv, rope, mask, ident, ot_dram, cs_dram):
    def sb(name, shape, dt=F32):
        return ctx.enter_context(nc.sbuf_tensor(name, shape, dt))

    def ps(name):
        return ctx.enter_context(nc.psum_tensor(name, [P, BANK], F32))

    def sem(name):
        return ctx.enter_context(nc.semaphore(name))

    w_sb = weights[:].rearrange("p (l g t n) -> p l g t n", l=2, g=NG, t=KT)

    xraw = sb("xraw", [P, 2, KT, S])
    xs = sb("xs", [P, 2, 2, KT, S], F32R)
    rope_t = sb("rope_t", [P, 2, 2, 1, DH])
    mask_t = sb("mask_t", [P, S])
    id_t = sb("id_t", [P, P])
    ones = sb("ones", [P, 32])
    rot1 = sb("rot1", [P, 2, BANK])
    rot2 = sb("rot2", [P, 2, BANK])
    qn = sb("qn", [P, NU, BANK])
    kx = sb("kx", [P, NU, NI, P])
    v_t = sb("v_t", [P, 2, KV])
    qt = sb("qt", [P, NU, 2, BANK], F32R)
    kt = sb("kt", [P, NU, 2, BANK], F32R)
    sm = sb("sm", [P, 2, BANK])
    smin = sb("smin", [P, 2, NI])
    pexp = sb("pexp", [P, 2, BANK])
    psum_row = sb("psum_row", [P, 2, NI])
    prec = sb("prec", [P, 2, NI])
    pn = sb("pn", [P, 2, BANK])
    pt = sb("pt", [P, NU, NI, NJ, S])
    ot = sb("ot", [P, NU, BANK])
    ctx_t = sb("ctx_t", [P, D])
    sq = sb("sq", [P, D])
    nb = sb("nb", [P, D])
    csum = sb("csum", [P, BANK])

    qkv_ps = [ps(f"qkv_ps{g}") for g in range(NG)]
    s_ps = ps("s_ps")
    turn_ps = ps("turn_ps")
    pt_ps = [ps("pt_ps0"), ps("pt_ps1")]
    o_ps = ps("o_ps")

    consts_in = sem("consts_in")
    w_in = [sem("w_in0"), sem("w_in1")]
    w_hi = sem("w_hi")
    w_lo = sem("w_lo")
    set_up = sem("set_up")
    x_in = [sem("x_in0"), sem("x_in1")]
    c_in = sem("c_in")
    x_hi = sem("x_hi")
    x_lo = sem("x_lo")
    qkv_done = sem("qkv_done")
    rope_read = sem("rope_read")
    roped = sem("roped")
    kx_turned = sem("kx_turned")
    kt_hi = sem("kt_hi")
    kt_lo = sem("kt_lo")
    q_turned = sem("q_turned")
    qt_hi = sem("qt_hi")
    qt_lo = sem("qt_lo")
    scored = sem("scored")
    masked = sem("masked")
    expd = sem("expd")
    inverted = sem("inverted")
    scaled = sem("scaled")
    p_turned = sem("p_turned")
    pt_read = sem("pt_read")
    pv_done = sem("pv_done")
    ot_read = sem("ot_read")
    ot_out = [sem("ot_out0"), sem("ot_out1")]
    sq_done = sem("sq_done")
    nb_done = sem("nb_done")
    summed = sem("summed")
    cs_read = sem("cs_read")
    cs_out = sem("cs_out")
    held = sem("held")

    LEAD, TAIL = 2, 3
    HK = KT // 2
    PIECES = 2 * NG

    block = ctx.enter_context(nc.Block())

    def stage(n):
        return pt[:, n % 2].rearrange("p i j s -> p (i j s)").rearrange("p (t n) -> p t n", t=HK)

    def w_piece(n, part):
        return w_sb[:, part, n // 2, (n % 2) * HK:(n % 2 + 1) * HK, :]

    @block.sync
    def _(sp):
        def load_x(t, par):
            wait(sp, x_lo, after(t - 2, 1, 1))
            sp.dma_start(xraw[:, par], xT[t]).then_inc(x_in[par], 16)

        def load_ctx(t):
            wait(sp, sq_done, after(t - 1, 1, 1))
            wait(sp, nb_done, after(t - 1, 1, 1))
            sp.dma_start(ctx_t[:], ctx_in[t]).then_inc(c_in, 16)

        sp.dma_start(xraw[:, 0], xT[0]).then_inc(x_in[0], 16)
        for n in range(PIECES):
            wait(sp, w_lo, n - 1)
            sp.dma_start(stage(n), wqkv[n // 2, :, (n % 2) * HK:(n % 2 + 1) * HK, :]).then_inc(w_in[n % 2], 16)
            if n == 1:
                sp.dma_start(rope_t[:], rope).then_inc(consts_in, 16)
                sp.dma_start(mask_t[:], mask).then_inc(consts_in, 16)
                sp.dma_start(id_t[:], ident).then_inc(consts_in, 16)
                load_ctx(0)

        def step(t, par):
            a = t - 1
            if valid(t + 1):
                load_x(t + 1, 1 - par)
                load_ctx(t + 1)
            if valid(a):
                wait(sp, ot_read, after(a, NU, 1))
                sp.dma_start(ot_dram[a, :, 0:BANK], ot[:, 0]).then_inc(ot_out[0], 16)
            if valid(t):
                wait(sp, cs_read, after(t, 1, 1))
                sp.dma_start(cs_dram[t], csum[0:P:32, :]).then_inc(cs_out, 16)
            if valid(a):
                wait(sp, ot_read, after(a, NU, 2))
                sp.dma_start(ot_dram[a, :, BANK:D], ot[:, 1]).then_inc(ot_out[1], 16)

        steps(sp, step, 0, B, LEAD, TAIL)
        sp.wait_ge(cs_out, 16 * B)
        for u in range(NU):
            sp.wait_ge(ot_out[u], 16 * B)

    @block.tensor
    def _(pe):
        def project(t, par, g, k):
            if g == 0 and k == 0:
                wait(pe, x_lo, after(t, 1, 1))
            if k == 0:
                wait(pe, rope_read, after(t - 1, NG, g + 1))
            if isinstance(t, int) and t == 0 and k % HK == 0:
                pe.wait_ge(w_lo, 2 * g + k // HK + 1)
            for n, (xl, wl) in enumerate(((0, 0), (0, 1), (1, 0))):
                mm = pe.matmul(qkv_ps[g][:], xs[:, par, xl, k], w_sb[:, wl, g, k],
                               start=(k == 0 and n == 0), stop=(k == KT - 1 and n == 2))
            if k == KT - 1:
                mm.then_inc(qkv_done, 1)

        def turn_k(t, u):
            wait(pe, roped, after(t, NG, 1))
            if u == 0:
                wait(pe, cs_read, after(t, 1, 1))
            else:
                wait(pe, kt_lo, after(t, NU, u))
            for i in range(NI):
                mm = pe.transpose(turn_ps[:, i * P:(i + 1) * P], kx[:, u, i], id_t[:])
            mm.then_inc(kx_turned, 1)

        def turn_q(t, u):
            wait(pe, roped, after(t, NG, 2 + u))
            if u == 0:
                wait(pe, kt_lo, after(t, NU, NU))
            else:
                wait(pe, qt_lo, after(t, NU, u))
            for j in range(NJ):
                mm = pe.transpose(turn_ps[:, j * P:(j + 1) * P], qn[:, u, j * P:(j + 1) * P], id_t[:])
            mm.then_inc(q_turned, 1)

        def score(a, c):
            u, j = divmod(c, NJ)
            wait(pe, qt_lo, after(a, NU, u + 1))
            wait(pe, kt_lo, after(a, NU, u + 1))
            wait(pe, masked, after(a, NC, c))
            for n, (ql, kl) in enumerate(((0, 0), (0, 1), (1, 0))):
                mm = pe.matmul(s_ps[:], qt[:, u, ql, j * P:(j + 1) * P], kt[:, u, kl],
                               start=(n == 0), stop=(n == 2))
            mm.then_inc(scored, 1)

        def turn_p(a, c):
            wait(pe, scaled, after(a, NC, c + 1))
            wait(pe, pt_read, after(a, NC, c - 1))
            for i in range(NI):
                mm = pe.transpose(pt_ps[c % 2][:, i * P:(i + 1) * P], pn[:, c % 2, i * P:(i + 1) * P], id_t[:])
            mm.then_inc(p_turned, 1)

        def weigh(a, par, u):
            wait(pe, pt_read, after(a, NC, NJ * (u + 1)))
            wait(pe, ot_read, after(a, NU, u))
            for i in range(NI):
                g = NI * u + i
                mm = pe.matmul(o_ps[32 * i:32 * i + 32, :], v_t[:, par, g * DH:(g + 1) * DH],
                               pt[:, u, i].rearrange("p j s -> p (j s)"), start=True, stop=True,
                               tile_position=(0, 32 * i))
            mm.then_inc(pv_done, 1)

        def sum_ctx(t):
            wait(pe, sq_done, after(t, 1, 1))
            wait(pe, nb_done, after(t, 1, 1))
            wait(pe, qt_lo, after(t - 1, NU, NU))
            for m in range(4):
                src = (sq, nb)[m // 2]
                mm = pe.matmul(turn_ps[32 * m:32 * m + 32, :], ones[:], src[:, (m % 2) * BANK:(m % 2 + 1) * BANK],
                               start=True, stop=True, tile_position=(0, 32 * m))
            mm.then_inc(summed, 1)

        pe.wait_ge(consts_in, 48)
        pe.wait_ge(set_up, 3)

        def step(t, par):
            a = t - 1
            for s in range(SLOTS):
                if valid(a):
                    if s % 2 == 0 and s // 2 < NC:
                        score(a, s // 2)
                    if s == 4:
                        turn_q(a, 1)
                    if s % 2 == 0 and 0 <= (s - 6) // 2 < NC:
                        turn_p(a, (s - 6) // 2)
                    if s == 15:
                        weigh(a, 1 - par, 0)
                    if s == 23:
                        weigh(a, 1 - par, 1)
                if valid(t):
                    if s == 12:
                        sum_ctx(t)
                    if s == 18:
                        turn_k(t, 0)
                    if s == 20:
                        turn_k(t, 1)
                    if s == 22:
                        turn_q(t, 0)
                    project(t, par, s // KT, s % KT)

        steps(pe, step, 0, B, LEAD, TAIL)

    @block.vector
    def _(dve):
        dve.memset(ones[:], 1.0).then_inc(set_up, 1)
        for n in range(PIECES):
            dve.wait_ge(w_in[n % 2], 16 * (n // 2 + 1))
            dve.tensor_copy(w_piece(n, 0), stage(n)).then_inc(w_hi, 1)
            dve.wait_ge(w_hi, n + 1)
            dve.tensor_tensor(w_piece(n, 1), stage(n), w_piece(n, 0).bitcast(F32), ALU.subtract).then_inc(w_lo, 1)

        def rotate(t, par, g):
            r = (par + g) % 2
            src, width = qkv_ps[g], KV if g == 0 else BANK
            tab = rope_t[:, 1 if g == 0 else 0]
            heads = width // DH
            wait(dve, qkv_done, after(t, NG, g + 1))
            wait(dve, roped, after(t, NG, g - 1))
            q3 = src[:, 0:width].rearrange("p (h d) -> p h d", d=DH)
            o1 = rot1[:, r, 0:width].rearrange("p (h d) -> p h d", d=DH)
            o2 = rot2[:, r, 0:width].rearrange("p (h d) -> p h d", d=DH)
            cos = tab[:, 0, 0].unsqueeze(1).broadcast_to([P, heads, DH])
            dve.tensor_tensor(o1, q3, cos, ALU.mult)
            for z in range(2):
                sin = tab[:, 1, 0, z * HALF:(z + 1) * HALF].unsqueeze(1).broadcast_to([P, heads, HALF])
                ins = dve.tensor_tensor(o2[:, :, z * HALF:(z + 1) * HALF],
                                        q3[:, :, (1 - z) * HALF:(2 - z) * HALF], sin, ALU.mult)
            if g == 0:
                wait(dve, pv_done, after(t - 2, NU, NU))
                ins = dve.tensor_copy(v_t[:, par], src[:, KV:2 * KV])
            ins.then_inc(rope_read, 1)

        def low_q(t, u):
            wait(dve, qt_hi, after(t, NU, u + 1))
            dve.tensor_tensor(qt[:, u, 1], turn_ps[:], qt[:, u, 0].bitcast(F32), ALU.subtract).then_inc(qt_lo, 1)

        def low_k(t, u):
            wait(dve, kt_hi, after(t, NU, u + 1))
            dve.tensor_tensor(kt[:, u, 1], turn_ps[:], kt[:, u, 0].bitcast(F32), ALU.subtract).then_inc(kt_lo, 1)

        def mask_min(a, c):
            wait(dve, scored, after(a, NC, c + 1))
            wait(dve, expd, after(a, NC, c - 1))
            dve.sem_inc(held)
            for i in range(NI):
                ins = dve.tensor_tensor_reduce(sm[:, c % 2, i * P:(i + 1) * P], s_ps[:, i * P:(i + 1) * P],
                                               mask_t[:], 1.0, 3e38, ALU.add, ALU.min, smin[:, c % 2, i:i + 1])
            ins.then_inc(masked, 1)

        def invert(a, c):
            wait(dve, expd, after(a, NC, c + 1))
            wait(dve, scaled, after(a, NC, c - 1))
            dve.reciprocal(prec[:, c % 2], psum_row[:, c % 2]).then_inc(inverted, 1)

        def read_pt(a, c):
            u, j = divmod(c, NJ)
            wait(dve, p_turned, after(a, NC, c + 1))
            wait(dve, pv_done, after(a - 1, NU, u + 1))
            dve.tensor_copy(pt[:, u, :, j], pt_ps[c % 2][:].rearrange("p (i s) -> p i s", i=NI)).then_inc(pt_read, 1)

        dve.wait_ge(consts_in, 48)

        def step(t, par):
            a = t - 1
            if valid(a):
                mask_min(a, 0)
                rotate(a, 1 - par, 2)
                mask_min(a, 1)
                invert(a, 0)
                low_q(a, 1)
                mask_min(a, 2)
                invert(a, 1)
                mask_min(a, 3)
                invert(a, 2)
                read_pt(a, 0)
                mask_min(a, 4)
                invert(a, 3)
                read_pt(a, 1)
            if valid(t):
                rotate(t, par, 0)
            if valid(a):
                mask_min(a, 5)
                invert(a, 4)
                read_pt(a, 2)
                mask_min(a, 6)
                invert(a, 5)
                read_pt(a, 3)
                mask_min(a, 7)
                invert(a, 6)
                read_pt(a, 4)
                invert(a, 7)
            if valid(t):
                rotate(t, par, 1)
            if valid(a):
                read_pt(a, 5)
            if valid(t):
                low_k(t, 0)
            if valid(a):
                read_pt(a, 6)
            if valid(t):
                low_k(t, 1)
            if valid(a):
                read_pt(a, 7)
            if valid(t):
                low_q(t, 0)

        steps(dve, step, 0, B, LEAD, TAIL)

    @block.scalar
    def _(act):
        def high_x(t, par):
            wait(act, x_in[par], arrivals(t, par))
            wait(act, qkv_done, after(t - 2, NG, NG))
            nc.scalar.copy(xs[:, par, 0], xraw[:, par]).then_inc(x_hi, 1)

        def square(t):
            wait(act, c_in, after(t, 16, 16))
            wait(act, summed, after(t - 1, 1, 1))
            nc.scalar.activation(sq[:], ctx_t[:], ACT.Square).then_inc(sq_done, 1)

        def high_q(t, u):
            wait(act, q_turned, after(t, NU, u + 1))
            wait(act, scored, after(t - 1, NC, NJ * (u + 1)))
            nc.scalar.copy(qt[:, u, 0], turn_ps[:]).then_inc(qt_hi, 1)

        def high_k(t, u):
            wait(act, kx_turned, after(t, NU, u + 1))
            wait(act, scored, after(t - 1, NC, NJ * (u + 1)))
            nc.scalar.copy(kt[:, u, 0], turn_ps[:]).then_inc(kt_hi, 1)

        def exponent(a, c):
            wait(act, masked, after(a, NC, c + 1))
            wait(act, scaled, after(a, NC, c - 1))
            wait(act, inverted, after(a, NC, c - 1))
            for i in range(NI):
                ins = nc.scalar.activation(pexp[:, c % 2, i * P:(i + 1) * P], sm[:, c % 2, i * P:(i + 1) * P],
                                           ACT.Exp, bias=smin[:, c % 2, i:i + 1], scale=-1.0,
                                           accum_out=psum_row[:, c % 2, i:i + 1])
            ins.then_inc(expd, 1)

        def read_ot(a, u):
            wait(act, pv_done, after(a, NU, u + 1))
            wait(act, ot_out[u], after(a, 16, 0))
            nc.scalar.copy(ot[:, u], o_ps[:]).then_inc(ot_read, 1)

        def read_sums(t):
            wait(act, summed, after(t, 1, 1))
            wait(act, cs_out, after(t, 16, 0))
            nc.scalar.copy(csum[:], turn_ps[:]).then_inc(cs_read, 1)

        high_x(0, 0)
        square(0)

        def step(t, par):
            a = t - 1
            if valid(a):
                exponent(a, 0)
                high_q(a, 1)
                exponent(a, 1)
            if valid(t + 1):
                high_x(t + 1, 1 - par)
            if valid(a):
                exponent(a, 2)
                exponent(a, 3)
                exponent(a, 4)
            if valid(t):
                read_sums(t)
            if valid(a):
                exponent(a, 5)
                exponent(a, 6)
            if valid(t + 1):
                square(t + 1)
            if valid(a):
                read_ot(a, 0)
                exponent(a, 7)
            if valid(t):
                high_k(t, 0)
                high_k(t, 1)
                high_q(t, 0)
            if valid(a):
                read_ot(a, 1)

        steps(act, step, 0, B, LEAD, TAIL)

    @block.gpsimd
    def _(pool):
        def low_x(t, par):
            wait(pool, x_hi, after(t, 1, 1))
            pool.tensor_tensor(xs[:, par, 1], xraw[:, par], xs[:, par, 0].bitcast(F32), ALU.subtract).then_inc(x_lo, 1)

        def neighbour(t):
            wait(pool, c_in, after(t, 16, 16))
            wait(pool, summed, after(t - 1, 1, 1))
            pool.tensor_tensor(nb[:, 0:D - 1], ctx_t[:, 0:D - 1], ctx_t[:, 1:D], ALU.mult).then_inc(nb_done, 1)

        def add_rope(t, par, g):
            r = (par + g) % 2
            width = KV if g == 0 else BANK
            wait(pool, rope_read, after(t, NG, g + 1))
            if g == 0:
                wait(pool, kx_turned, after(t - 1, NU, NU))
                for u in range(NU):
                    dst = diagonal(kx[:, u].rearrange("p i c -> p (i c)"))
                    cols = slice(u * P, (u + 1) * P)
                    ins = pool.tensor_tensor(dst, rot1[:, r, cols].rearrange("p (i d) -> p i d", d=DH),
                                             rot2[:, r, cols].rearrange("p (i d) -> p i d", d=DH), ALU.add)
            else:
                wait(pool, q_turned, after(t - 1, NU, g))
                ins = pool.tensor_tensor(qn[:, g - 1], rot1[:, r], rot2[:, r], ALU.add)
            ins.then_inc(roped, 1)

        def scale(a, c):
            wait(pool, inverted, after(a, NC, c + 1))
            wait(pool, p_turned, after(a, NC, c - 1))
            pool.tensor_tensor(pn[:, c % 2].rearrange("p (i s) -> p i s", i=NI),
                               pexp[:, c % 2].rearrange("p (i s) -> p i s", i=NI),
                               prec[:, c % 2].unsqueeze(2).broadcast_to([P, NI, S]), ALU.mult).then_inc(scaled, 1)

        pool.memset(kx[:], 0.0).then_inc(set_up, 1)
        pool.memset(nb[:, D - 1:D], 0.0).then_inc(set_up, 1)
        low_x(0, 0)
        neighbour(0)
        pool.wait_ge(set_up, 3)

        def step(t, par):
            a = t - 1
            if valid(a):
                add_rope(a, 1 - par, 2)
                scale(a, 0)
                scale(a, 1)
            if valid(t + 1):
                low_x(t + 1, 1 - par)
            if valid(a):
                scale(a, 2)
            if valid(t):
                add_rope(t, par, 0)
            if valid(a):
                scale(a, 3)
                scale(a, 4)
            if valid(t + 1):
                neighbour(t + 1)
            if valid(a):
                scale(a, 5)
                scale(a, 6)
            if valid(t):
                add_rope(t, par, 1)
            if valid(a):
                scale(a, 7)

        steps(pool, step, 0, B, LEAD, TAIL)


def diagonal(blocks):
    return bass.AP(tensor=blocks.tensor, offset=blocks.offset,
                   ap=[list(blocks.ap[0]), [P + DH, NI], [1, DH]])


def part2(nc, ctx, weights, x, wo, wx, wa, wb, br, ident, tapsel, ot_dram, cs_dram, sim_dram, out):
    def sb(name, shape, dt=F32):
        return ctx.enter_context(nc.sbuf_tensor(name, shape, dt))

    def ps(name):
        return ctx.enter_context(nc.psum_tensor(name, [P, BANK], F32))

    def sem(name):
        return ctx.enter_context(nc.semaphore(name))

    sizes = {"wo": 2 * KT * D, "wa": KT * 2 * LOWW, "wb": 2 * D, "wx": 2 * TAPS * P, "sel": TAPS * P}
    at, offset = {}, 0
    for name, size in sizes.items():
        at[name] = weights[:, offset:offset + size]
        offset += size
    wo_sb = at["wo"].rearrange("p (l t n) -> p l t n", l=2, t=KT)
    wa_sb = at["wa"].rearrange("p (t l n) -> p t l n", t=KT, l=2)
    wb_sb = at["wb"].rearrange("p (l n) -> p l n", l=2)
    wx_sb = at["wx"].rearrange("p (l k o) -> p l k o", l=2, k=TAPS)
    sel_sb = at["sel"].rearrange("p (k c) -> p k c", k=TAPS)

    oraw = sb("oraw", [P, 2, D])
    os_t = sb("os_t", [P, 2, 2, KT, S], F32R)
    xn = sb("xn", [P, 2, D])
    yz = sb("yz", [P, 2, D])
    y3 = sb("y3", [P, D])
    x1 = sb("x1", [P, 2, D + 2])
    sim = sb("sim", [P, 2, D], F32R)
    prod = sb("prod", [P, 2, BANK])
    prods = sb("prods", [P, 2, 2, BANK], F32R)
    late = sb("late", [P, 2, 2, D])
    xt = sb("xt", [P, 2, KT, S], F32R)
    br_t = sb("br_t", [P, H])
    id_t = sb("id2_t", [P, P])
    lowhi = sb("lowhi", [P, LOWW])
    low = sb("low", [P, LOWW])
    logit = sb("logit", [P, H])
    nmax = sb("nmax", [P, 1])
    gate = sb("gate", [P, H])
    gsum = sb("gsum", [P, 1])
    grec = sb("grec", [P, 1])
    gated = sb("gated", [P, HR])
    lt = sb("lt", [P, 2, S], F32R)
    power = sb("power", [P, 1])
    stats = [sb(f"stats{n}", [P, 2, 6]) for n in range(3)]
    mv = [sb(f"mv{n}", [P, 2]) for n in range(3)]
    var = [sb(f"var{n}", [P, 1]) for n in range(3)]
    rstd = [sb(f"rstd{n}", [P, 1]) for n in range(3)]

    x2, res = late[:, 0], late[:, 1]
    wo_ps = [ps("wo_ps0"), ps("wo_ps1")]
    att_ps = [ps("att_ps0"), ps("att_ps1")]
    conv_ps = [ps("conv_ps0"), ps("conv_ps1")]
    ffn_ps = [ps("ffn_ps0"), ps("ffn_ps1")]

    consts_in = sem("consts2_in")
    w_in = [sem("w2_in0"), sem("w2_in1")]
    w_hi = sem("w2_hi")
    w_lo = sem("w2_lo")
    set_up = sem("set_up2")
    cs_in = sem("cs_in")
    root = sem("root")
    cos_step = sem("cos_step")
    sim_made = sem("sim_made")
    sim_out = sem("sim_out")
    o_in = [sem("o_in0"), sem("o_in1")]
    xn_in = [sem("xn_in0"), sem("xn_in1")]
    sim_in = [sem("sim_in0"), sem("sim_in1")]
    o_hi = sem("o_hi")
    o_lo = sem("o_lo")
    wo_done = sem("wo_done")
    added = [sem(f"added{n}") for n in range(3)]
    counted = [sem(f"counted{n}") for n in range(3)]
    averaged = [sem(f"averaged{n}") for n in range(3)]
    var_done = [sem(f"var_done{n}") for n in range(3)]
    rstd_done = [sem(f"rstd_done{n}") for n in range(3)]
    normed = [sem(f"normed{n}") for n in range(3)]
    att_done = sem("att_done")
    prod_done = sem("prod_done")
    prod_hi = sem("prod_hi")
    prod_lo = sem("prod_lo")
    conv_done = sem("conv_done")
    x2_turned = sem("x2_turned")
    xt_hi = sem("xt_hi")
    xt_lo = sem("xt_lo")
    low_done = sem("low_done")
    low_step = sem("low_step")
    gate_in = sem("gate_in")
    gate_done = sem("gate_done")
    gated_done = sem("gated_done")
    low_turned = sem("low_turned")
    lt_hi = sem("lt_hi")
    lt_lo = sem("lt_lo")
    ffn_done = sem("ffn_done")
    held = sem("held2")
    stored = [sem("stored0"), sem("stored1")]

    LAST = B + 2
    LEAD, TAIL = 4, 5
    UNITS = 2 * TAPS
    SLOTS2 = 2 * KT
    WO_PIECES, WO_KT = 4, KT // 4
    PIECES = WO_PIECES + 2
    LOWCHAIN = 4

    stage = [late[:, n].rearrange("p a d -> p (a d)") for n in range(2)]
    misc = {"wa": slice(0, KT * LOWW), "wx": slice(KT * LOWW, KT * LOWW + TAPS * P),
            "sel": slice(KT * LOWW + TAPS * P, KT * LOWW + 2 * TAPS * P)}
    simparts = prods[:].rearrange("p a l n -> p (a l n)").rearrange("p (l t) -> p l t", l=2)

    block = ctx.enter_context(nc.Block())

    @block.sync
    def _(sp):
        def load_o(t, par):
            wait(sp, o_lo, after(t - 2, 1, 1))
            sp.dma_start(oraw[:, par], ot_dram[t]).then_inc(o_in[par], 16)
            wait(sp, added[0], after(t - 2, 2, 2))
            sp.dma_start(xn[:, par], x[t]).then_inc(xn_in[par], 16)

        def load_sim(t, par):
            wait(sp, att_done, after(t - 2, UNITS, UNITS))
            sp.dma_start(sim[0:2 * TAPS, par].bitcast(F32), sim_dram[t]).then_inc(sim_in[par], 16)

        sp.dma_start(yz[0:B].rearrange("p a d -> p (a d)"), cs_dram.rearrange("b q n -> b (q n)")).then_inc(cs_in, 16)
        for n in range(PIECES):
            wait(sp, w_lo, n - 1)
            if n < WO_PIECES:
                sp.dma_start(stage[n % 2].rearrange("p (t n) -> p t n", t=WO_KT),
                             wo[:, n * WO_KT:(n + 1) * WO_KT, :]).then_inc(w_in[n % 2], 16)
            elif n == WO_PIECES:
                sp.dma_start(stage[0][:, misc["wa"]], wa).then_inc(w_in[0], 16)
                sp.dma_start(stage[0][:, misc["wx"]], wx).then_inc(w_in[0], 16)
                sp.dma_start(stage[0][:, misc["sel"]], tapsel).then_inc(w_in[0], 16)
            else:
                sp.dma_start(stage[1][:, 0:D], wb).then_inc(w_in[1], 16)
            if n == 0:
                load_o(0, 0)
                sp.dma_start(id_t[:], ident).then_inc(consts_in, 16)
                sp.dma_start(br_t[:], br).then_inc(consts_in, 16)
        for n, m in enumerate((1, 2, 0)):
            sp.wait_ge(sim_made, n + 1)
            for part in range(2):
                sp.dma_start(sim_dram[:, part * TAPS + m, :], simparts[0:B, part].bitcast(F32)).then_inc(sim_out, 16)
        sp.wait_ge(sim_out, 16 * 2 * TAPS)
        sp.wait_ge(set_up, 4)

        def step(t, par):
            if valid(t + 1):
                load_o(t + 1, 1 - par)
            if valid(t):
                load_sim(t, par)
            if valid(t - 3):
                wait(sp, normed[2], after(t - 3, 1, 1))
                sp.dma_start(out[t - 3], res[:, 1 - par]).then_inc(stored[1 - par], 16)

        steps(sp, step, 0, LAST, LEAD, TAIL)
        for par in range(2):
            sp.wait_ge(stored[par], 16 * B // 2)

    @block.tensor
    def _(pe):
        def project(t, par, n, k):
            if n == 0 and k == 0:
                wait(pe, o_lo, after(t, 1, 1))
            if k == 0:
                wait(pe, added[0], after(t - 1, 2, n + 1))
            for m, (ol, wl) in enumerate(((0, 0), (0, 1), (1, 0))):
                mm = pe.matmul(wo_ps[n][:], os_t[:, par, ol, k], wo_sb[:, wl, k, n * BANK:(n + 1) * BANK],
                               start=(k == 0 and m == 0), stop=(k == KT - 1 and m == 2))
            if k == KT - 1:
                mm.then_inc(wo_done, 1)

        def spread(t, par, m):
            h, k = divmod(m, TAPS)
            if m == 0:
                wait(pe, sim_in[par], arrivals(t, par))
            wait(pe, prod_done, after(t, UNITS, m - 1))
            pe.matmul(att_ps[m % 2][:], sel_sb[:, k], sim[:, par, h * BANK:(h + 1) * BANK],
                      start=True, stop=True).then_inc(att_done, 1)

        def convolve(t, m):
            h, k = divmod(m, TAPS)
            wait(pe, prod_lo, after(t, UNITS, m + 1))
            if k == 0:
                wait(pe, added[1], after(t - 1, 2, h + 1))
            for n, (wl, xl) in enumerate(((0, 0), (1, 0), (0, 1))):
                mm = pe.matmul(conv_ps[h][:], wx_sb[:, wl, k], prods[:, m % 2, xl],
                               start=(k == 0 and n == 0), stop=(k == TAPS - 1 and n == 2))
            mm.then_inc(conv_done, 1)

        def turn_x2(t, par, n):
            wait(pe, normed[1], after(t, 1, 1))
            wait(pe, added[2], after(t - 1, 2, n + 1))
            for k in range(NJ):
                c = (n * NJ + k) * P
                mm = pe.transpose(ffn_ps[n][:, k * P:(k + 1) * P], x2[:, par, c:c + P], id_t[:])
            mm.then_inc(x2_turned, 1)

        def reduce_rank(t):
            wait(pe, xt_lo, after(t, 2, 2))
            for k in range(KT):
                for xl in range(2):
                    mm = pe.matmul(ffn_ps[0][:, 0:2 * LOWW], xt[:, xl, k],
                                   wa_sb[:, k].rearrange("p l n -> p (l n)"),
                                   start=(k == 0 and xl == 0), stop=(k == KT - 1 and xl == 1))
            mm.then_inc(low_done, 1)

        def turn_low(t):
            wait(pe, gated_done, after(t, 1, 1))
            pe.transpose(ffn_ps[1][:, 0:S], gated[:], id_t[:]).then_inc(low_turned, 1)

        def expand(t):
            wait(pe, lt_lo, after(t, 1, 1))
            for n in range(2):
                for m, (ll, wl) in enumerate(((0, 0), (0, 1), (1, 0))):
                    mm = pe.matmul(ffn_ps[n][:], lt[:, ll], wb_sb[:, wl, n * BANK:(n + 1) * BANK],
                                   start=(m == 0), stop=(m == 2))
                mm.then_inc(ffn_done, 1)

        pe.wait_ge(consts_in, 32)
        pe.wait_ge(set_up, 4)
        pe.wait_ge(w_lo, PIECES)

        def step(t, par):
            for s in range(SLOTS2):
                if valid(t - 1):
                    if s % 2 == 0 and s // 2 < UNITS:
                        spread(t - 1, 1 - par, s // 2)
                    if s % 2 == 1 and 0 <= (s - 5) // 2 < UNITS:
                        convolve(t - 1, (s - 5) // 2)
                if valid(t - 2):
                    if s in (4, 5):
                        turn_x2(t - 2, par, s - 4)
                    if s == 8:
                        reduce_rank(t - 2)
                    if s == 12:
                        turn_low(t - 2)
                    if s == 15:
                        expand(t - 2)
                if valid(t):
                    project(t, par, s // KT, s % KT)

        steps(pe, step, 0, LAST, LEAD, TAIL)

    @block.vector
    def _(dve):
        dve.memset(power[:], -0.5).then_inc(set_up, 1)
        dve.memset(x1[:, :, 0:1], 0.0).then_inc(set_up, 1)
        dve.memset(x1[:, :, D + 1:D + 2], 0.0).then_inc(set_up, 1)
        dve.memset(sim[:].bitcast(F32), 0.0).then_inc(set_up, 1)

        def split(n, hi, lo, src):
            dve.tensor_copy(hi, src).then_inc(w_hi, 1)
            dve.wait_ge(w_hi, n + 1)
            return dve.tensor_tensor(lo, src, hi.bitcast(F32), ALU.subtract)

        for n in range(WO_PIECES):
            dve.wait_ge(w_in[n % 2], 16 * (n // 2 + 1))
            k = slice(n * WO_KT, (n + 1) * WO_KT)
            split(n, wo_sb[:, 0, k], wo_sb[:, 1, k],
                  stage[n % 2].rearrange("p (t n) -> p t n", t=WO_KT)).then_inc(w_lo, 1)
        dve.wait_ge(w_in[0], 16 * (WO_PIECES // 2 + 3))
        raw = stage[0][:, misc["wa"]].rearrange("p (t n) -> p t n", t=KT)
        split(WO_PIECES, wa_sb[:, :, 0], wa_sb[:, :, 1], raw)
        raw = stage[0][:, misc["wx"]].rearrange("p (k o) -> p k o", k=TAPS)
        split(WO_PIECES + 1, wx_sb[:, 0], wx_sb[:, 1], raw)
        raw = stage[0][:, misc["sel"]].rearrange("p (k c) -> p k c", k=TAPS)
        dve.tensor_copy(sel_sb, raw).then_inc(w_lo, 1)
        dve.wait_ge(w_in[1], 16 * (WO_PIECES // 2 + 1))
        split(WO_PIECES + 2, wb_sb[:, 0], wb_sb[:, 1], stage[1][:, 0:D]).then_inc(w_lo, 1)

        sqs, nbs, norm = yz[0:B, 0], yz[0:B, 1], y3[0:B]
        value = prod[0:B].rearrange("p a n -> p (a n)")
        done = 0

        def chain(ins):
            ins.then_inc(cos_step, 1)
            dve.wait_ge(cos_step, done + 1)
            return done + 1

        def publish(n, first, width):
            if n:
                dve.wait_ge(sim_out, 32 * n)
            dst = slice(first, first + width)
            at_end = dve.tensor_copy(simparts[0:B, 0, dst], value[:, 0:width])
            d = chain(at_end)
            return d, dve.tensor_tensor(simparts[0:B, 1, dst], value[:, 0:width],
                                        simparts[0:B, 0, dst].bitcast(F32), ALU.subtract)

        dve.wait_ge(root, 1)
        done = chain(dve.tensor_scalar(norm, norm, COS_EPS, None, ALU.max))
        done = chain(dve.tensor_tensor(value, norm, norm, ALU.mult))
        done = chain(dve.reciprocal(value, value))
        done = chain(dve.tensor_tensor(value, value, sqs, ALU.mult))
        done, ins = publish(0, 0, D)
        ins.then_inc(sim_made, 1)
        dve.wait_ge(sim_made, 1)
        dve.tensor_copy(value[:, D - 1:D], norm[:, D - 1:D])
        done = chain(dve.tensor_tensor(value[:, 0:D - 1], norm[:, 0:D - 1], norm[:, 1:D], ALU.mult))
        done = chain(dve.reciprocal(value, value))
        done = chain(dve.tensor_tensor(value, value, nbs, ALU.mult))
        done, ins = publish(1, 0, D)
        ins.then_inc(sim_made, 1)
        dve.wait_ge(sim_out, 64)
        dve.memset(simparts[0:B, :, 0:1].bitcast(F32), 0.0)
        done, ins = publish(2, 1, D - 1)
        ins.then_inc(sim_made, 1)

        def add(t, par, n, half):
            cols = slice(half * BANK, (half + 1) * BANK)
            if n == 0:
                wait(dve, wo_done, after(t, 2, half + 1))
                if half == 0:
                    wait(dve, xn_in[par], arrivals(t, par))
                dst = yz[:, 0, cols]
                ins = dve.tensor_tensor(dst, wo_ps[half][:], xn[:, par, cols], ALU.add)
            elif n == 1:
                wait(dve, conv_done, after(t, UNITS, TAPS * (half + 1)))
                dst = yz[:, 1, cols]
                ins = dve.tensor_tensor(dst, conv_ps[half][:], x1[:, par, 1 + half * BANK:1 + (half + 1) * BANK], ALU.add)
            else:
                wait(dve, ffn_done, after(t, 2, half + 1))
                dst = y3[:, cols]
                ins = dve.scalar_tensor_tensor(dst, ffn_ps[half][:], FFN_SCALE, x2[:, par, cols], ALU.mult, ALU.add)
            ins.then_inc(added[n], 1)
            dve.wait_ge(added[n], after(t, 2, half + 1))
            dve.bn_stats(stats[n][:, half], dst).then_inc(counted[n], 1)

        def average(t, n):
            dve.wait_ge(counted[n], after(t, 2, 2))
            dve.sem_inc(held)
            dve.bn_aggr(mv[n][:], stats[n][:]).then_inc(averaged[n], 1)
            dve.wait_ge(averaged[n], after(t, 1, 1))
            dve.tensor_scalar(var[n][:], mv[n][:, 1:2], LN_EPS, None, ALU.add).then_inc(var_done[n], 1)

        def normalise(t, par, n):
            src = y3[:] if n == 2 else yz[:, n]
            dst = (x1[:, par, 1:D + 1], x2[:, par], res[:, par])[n]
            wait(dve, rstd_done[n], after(t, 1, 1))
            if n == 2:
                wait(dve, stored[par], arrivals(t, par) - 16)
            dve.tensor_scalar(dst, src, mv[n][:, 0:1], rstd[n][:], ALU.subtract, ALU.mult).then_inc(normed[n], 1)

        def multiply(t, par, m):
            h, k = divmod(m, TAPS)
            wait(dve, att_done, after(t, UNITS, m + 1))
            wait(dve, prod_lo, after(t, UNITS, m - 1))
            if m == 0:
                dve.wait_ge(normed[0], after(t, 1, 1))
            dve.tensor_tensor(prod[:, m % 2], att_ps[m % 2][:],
                              x1[:, par, h * BANK + k:h * BANK + k + BANK], ALU.mult).then_inc(prod_done, 1)

        def low_x2(t, n):
            wait(dve, xt_hi, after(t, 2, n + 1))
            dst = xt[:, :, n * NJ:(n + 1) * NJ].rearrange("p l t s -> p l (t s)")
            dve.tensor_tensor(dst[:, 1], ffn_ps[n][:], dst[:, 0].bitcast(F32), ALU.subtract).then_inc(xt_lo, 1)

        def route(t):
            wait(dve, low_done, after(t, 1, 1))
            dve.tensor_copy(lowhi[:], ffn_ps[0][:, LOWW:2 * LOWW]).then_inc(low_step, 1)
            dve.wait_ge(low_step, after(t, LOWCHAIN, 1))
            dve.tensor_tensor(low[:], ffn_ps[0][:, 0:LOWW], lowhi[:], ALU.add).then_inc(low_step, 1)
            dve.wait_ge(low_step, after(t, LOWCHAIN, 2))
            dve.tensor_tensor(logit[:], low[:, HR:LOWW], br_t[:], ALU.add).then_inc(low_step, 1)
            dve.wait_ge(low_step, after(t, LOWCHAIN, 3))
            dve.tensor_reduce(nmax[:], logit[:], AX.X, ALU.max, negate=True).then_inc(gate_in, 1)

        def gate_low(t):
            wait(dve, gate_done, after(t, 1, 1))
            dve.reciprocal(grec[:], gsum[:]).then_inc(low_step, 1)
            dve.wait_ge(low_step, after(t, LOWCHAIN, 4))
            dve.scalar_tensor_tensor(gated[:].rearrange("p (h r) -> p h r", h=H),
                                     low[:, 0:HR].rearrange("p (h r) -> p h r", h=H), grec[:],
                                     gate[:].unsqueeze(2).broadcast_to([P, H, R]),
                                     ALU.mult, ALU.mult).then_inc(gated_done, 1)

        def low_lt(t):
            wait(dve, lt_hi, after(t, 1, 1))
            dve.tensor_tensor(lt[:, 1], ffn_ps[1][:, 0:S], lt[:, 0].bitcast(F32), ALU.subtract).then_inc(lt_lo, 1)

        dve.wait_ge(consts_in, 32)
        dve.wait_ge(sim_out, 96)

        def step(t, par):
            c, f, z = t - 1, t - 2, t - 3
            if valid(c):
                add(c, 1 - par, 0, 1)
                average(c, 0)
            if valid(f):
                add(f, par, 1, 1)
                average(f, 1)
            if valid(c):
                normalise(c, 1 - par, 0)
                multiply(c, 1 - par, 0)
            if valid(f):
                normalise(f, par, 1)
            if valid(z):
                add(z, 1 - par, 2, 0)
                add(z, 1 - par, 2, 1)
            if valid(c):
                multiply(c, 1 - par, 1)
            if valid(z):
                average(z, 2)
            if valid(f):
                low_x2(f, 0)
            if valid(c):
                multiply(c, 1 - par, 2)
            if valid(z):
                normalise(z, 1 - par, 2)
            if valid(f):
                low_x2(f, 1)
            if valid(t):
                add(t, par, 0, 0)
            if valid(c):
                multiply(c, 1 - par, 3)
            if valid(f):
                route(f)
            if valid(c):
                multiply(c, 1 - par, 4)
            if valid(f):
                gate_low(f)
            if valid(c):
                add(c, 1 - par, 1, 0)
                multiply(c, 1 - par, 5)
            if valid(f):
                low_lt(f)

        steps(dve, step, 0, LAST, LEAD, TAIL)

    @block.scalar
    def _(act):
        act.wait_ge(cs_in, 16)
        nc.scalar.activation(y3[0:B], yz[0:B, 0], ACT.Sqrt).then_inc(root, 1)

        def high_o(t, par):
            wait(act, o_in[par], arrivals(t, par))
            wait(act, wo_done, after(t - 2, 2, 2))
            nc.scalar.copy(os_t[:, par, 0].rearrange("p t s -> p (t s)"), oraw[:, par]).then_inc(o_hi, 1)

        def high_prod(t, m):
            wait(act, prod_done, after(t, UNITS, m + 1))
            wait(act, conv_done, after(t, UNITS, m - 1))
            nc.scalar.copy(prods[:, m % 2, 0], prod[:, m % 2]).then_inc(prod_hi, 1)

        def high_x2(t, n):
            wait(act, x2_turned, after(t, 2, n + 1))
            wait(act, low_done, after(t - 1, 1, 1))
            nc.scalar.copy(xt[:, 0, n * NJ:(n + 1) * NJ].rearrange("p t s -> p (t s)"),
                           ffn_ps[n][:]).then_inc(xt_hi, 1)

        def gates(t):
            wait(act, gate_in, after(t, 1, 1))
            wait(act, gated_done, after(t - 1, 1, 1))
            nc.scalar.activation(gate[:], logit[:], ACT.Exp, bias=nmax[:], accum_out=gsum[:]).then_inc(gate_done, 1)

        def high_lt(t):
            wait(act, low_turned, after(t, 1, 1))
            wait(act, ffn_done, after(t - 1, 2, 2))
            nc.scalar.copy(lt[:, 0], ffn_ps[1][:, 0:S]).then_inc(lt_hi, 1)

        high_o(0, 0)
        act.wait_ge(sim_out, 96)

        def step(t, par):
            c, f = t - 1, t - 2
            if valid(c):
                high_prod(c, 0)
            if valid(f):
                high_x2(f, 0)
                high_x2(f, 1)
            if valid(c):
                high_prod(c, 1)
                high_prod(c, 2)
            if valid(t + 1):
                high_o(t + 1, 1 - par)
            if valid(c):
                high_prod(c, 3)
            if valid(f):
                gates(f)
            if valid(c):
                high_prod(c, 4)
                high_prod(c, 5)
            if valid(f):
                high_lt(f)

        steps(act, step, 0, LAST, LEAD, TAIL)

    @block.gpsimd
    def _(pool):
        def low_o(t, par):
            wait(pool, o_hi, after(t, 1, 1))
            hi, lo = (os_t[:, par, part].rearrange("p t s -> p (t s)") for part in range(2))
            pool.tensor_tensor(lo, oraw[:, par], hi.bitcast(F32), ALU.subtract).then_inc(o_lo, 1)

        def invert_root(t, n):
            wait(pool, var_done[n], after(t, 1, 1))
            wait(pool, normed[n], after(t - 1, 1, 1))
            pool.tensor_tensor(rstd[n][:], var[n][:], power[:], ALU.pow).then_inc(rstd_done[n], 1)

        def low_prod(t, m):
            wait(pool, prod_hi, after(t, UNITS, m + 1))
            pool.tensor_tensor(prods[:, m % 2, 1], prod[:, m % 2], prods[:, m % 2, 0].bitcast(F32),
                               ALU.subtract).then_inc(prod_lo, 1)

        low_o(0, 0)
        pool.wait_ge(set_up, 4)

        def step(t, par):
            c, f, z = t - 1, t - 2, t - 3
            if valid(c):
                invert_root(c, 0)
            if valid(f):
                invert_root(f, 1)
            if valid(c):
                low_prod(c, 0)
                low_prod(c, 1)
            if valid(z):
                invert_root(z, 2)
            if valid(c):
                low_prod(c, 2)
            if valid(t + 1):
                low_o(t + 1, 1 - par)
            if valid(c):
                for m in range(3, UNITS):
                    low_prod(c, m)

        steps(pool, step, 0, LAST, LEAD, TAIL)


def rope_tables():
    inv = np.float32(1.0) / np.float32(10000.0) ** (np.arange(0, DH, 2, dtype=np.float32) / np.float32(DH))
    angle = np.arange(S, dtype=np.float32)[:, None] * inv[None, :].astype(np.float32)
    cos = np.concatenate([np.cos(angle)] * 2, axis=1)
    sin = np.concatenate([-np.sin(angle), np.sin(angle)], axis=1)
    scale = np.array([-float(DH) ** -0.5, 1.0])
    tab = scale[None, :, None, None] * np.stack([cos, sin], axis=1)[:, None]
    return np.ascontiguousarray(tab.astype(np.float32).reshape(S, 2, 2, 1, DH))


def tap_selectors():
    sel = np.zeros((P, TAPS, S), np.float32)
    for k in range(TAPS):
        m = (TAPS * np.arange(S) + k) // S
        for part in range(2):
            sel[part * TAPS + m, k, np.arange(S)] = 1.0
    return sel.reshape(P, TAPS * S)


def kernel(**inputs):
    import concourse.bacc as bacc
    from concourse.bass_utils import run_bass_kernel_spmd

    f = {k: np.asarray(v) for k, v in inputs.items()}
    heads = (NU, NI, NJ, DH)
    q = f["L0_attn_wq"].reshape(*heads, D).transpose(0, 2, 1, 3, 4).reshape(D, D)
    cols = np.concatenate([f["L0_attn_wk"], f["L0_attn_wv"], q]).reshape(NG, BANK, KT, P)
    low = np.concatenate([f["L0_ffn_A"].reshape(HR, D), f["L0_ffn_Wr"]]).reshape(LOWW, KT, P)
    keys = np.arange(S)
    arrays = {
        "xT": f["x"].reshape(B, S, KT, P).transpose(0, 3, 2, 1),
        "x": f["x"],
        "ctx": f["ctx_4096"],
        "wqkv": cols.transpose(0, 3, 2, 1),
        "wo": f["L0_attn_wo"].reshape(D, *heads).transpose(2, 4, 1, 3, 0).reshape(P, KT, D),
        "wx": f["L0_xattn_weight"].transpose(1, 2, 0).reshape(S, TAPS * S),
        "wa": low.transpose(2, 1, 0).reshape(P, KT * LOWW),
        "wb": f["L0_ffn_B"].transpose(0, 2, 1).reshape(HR, D),
        "br": np.broadcast_to(f["L0_ffn_br"], (P, H)),
        "rope": rope_tables(),
        "mask": np.where(keys[None, :] > keys[:, None], np.float32(MASKED), np.float32(0.0)),
        "ident": np.eye(P, dtype=np.float32),
        "tapsel": tap_selectors(),
    }
    arrays = {f"in_{k}": np.ascontiguousarray(v) for k, v in arrays.items()}
    nc = bacc.Bacc("TRN2", target_bir_lowering=False, num_devices=1)
    args = [nc.dram_tensor(k, v.shape, mybir.dt.from_np(v.dtype), kind="ExternalInput").ap()
            for k, v in arrays.items()]
    out = nc.dram_tensor("out", (B, S, D), F32, kind="ExternalOutput").ap()
    build(nc, *args, out)
    r = run_bass_kernel_spmd(nc, [arrays], core_ids=[0])
    return r.results[0]["out"]
```

```python
from contextlib import ExitStack

import numpy as np

import concourse.bass as bass
from concourse import mybir

F32 = mybir.dt.float32
F32R = mybir.dt.float32r
ALU = mybir.AluOpType
ACT = mybir.ActivationFunctionType
AX = mybir.AxisListType

B, S, D = 32, 128, 1024
P = 128
KT = D // P
HEADS, KVH, DH = 32, 8, 32
NU = 2
NI = KVH // NU
NJ = HEADS // KVH
NC = NU * NJ
HALF = DH // 2
BANK = 512
KV = KVH * DH
NG = 3
SLOTS = NG * KT
R, H = 16, 8
HR = H * R
LOWW = HR + H
FFN_SCALE = float(H) * 2.0
LN_EPS = 1e-5
COS_EPS = 1e-8
MASKED = 1e30
TAPS = 3


def after(t, per, k):
    return t * per + k


def arrivals(t, par):
    return (t - par) * (16 // 2) + 16


def wait(eng, sem, count):
    if isinstance(count, int) and count <= 0:
        return
    eng.wait_ge(sem, count)


def valid(t):
    return not isinstance(t, int) or 0 <= t < B


def steps(eng, step, first, last, lead, tail):
    lo, hi = first + lead, last - tail + 1
    assert lo % 2 == 0 and hi % 2 == 0
    for t in range(first, lo):
        step(t, t % 2)
    with eng.Fori(lo // 2, hi // 2) as i:
        step(i * 2, 0)
        step(i * 2 + 1, 1)
    for t in range(hi, last + 1):
        step(t, t % 2)


def later_weights(weights):
    sizes = {"wo": 2 * KT * D, "wa": KT * 2 * LOWW, "wb": 2 * D, "wx": 2 * TAPS * P, "sel": TAPS * P}
    at, offset = {}, 0
    for name, size in sizes.items():
        at[name] = weights[:, offset:offset + size]
        offset += size
    return (at["wo"].rearrange("p (l t n) -> p l t n", l=2, t=KT),
            at["wa"].rearrange("p (t l n) -> p t l n", t=KT, l=2),
            at["wb"].rearrange("p (l n) -> p l n", l=2),
            at["wx"].rearrange("p (l n) -> p l n", l=2),
            at["sel"])


def build(nc, xT, x, ctx_in, wqkv, wo, wx, wa, wb, br, rope, mask, ident, tapsel, out):
    ot_dram = nc.dram_tensor("ot_scratch", [B, P, D], F32, kind="Internal").ap()
    cs_dram = nc.dram_tensor("cs_scratch", [B, 4, BANK], F32, kind="Internal").ap()
    sim_dram = nc.dram_tensor("sim_scratch", [B, 4, D], F32, kind="Internal").ap()
    with ExitStack() as both:
        weights = both.enter_context(nc.sbuf_tensor("weights", [P, 2 * NG * KT * BANK], F32R))
        with ExitStack() as ctx:
            part1(nc, ctx, weights, xT, ctx_in, wqkv, wo, wx, wa, wb, tapsel, rope, mask, ident,
                  ot_dram, cs_dram, sim_dram)
        with ExitStack() as ctx:
            part2(nc, ctx, weights, x, br, ident, ot_dram, sim_dram, out)


def part1(nc, ctx, weights, xT, ctx_in, wqkv, wo, wx, wa, wb, tapsel, rope, mask, ident,
          ot_dram, cs_dram, sim_dram):
    def sb(name, shape, dt=F32):
        return ctx.enter_context(nc.sbuf_tensor(name, shape, dt))

    def ps(name):
        return ctx.enter_context(nc.psum_tensor(name, [P, BANK], F32))

    def sem(name):
        return ctx.enter_context(nc.semaphore(name))

    w_sb = weights[:].rearrange("p (l g t n) -> p l g t n", l=2, g=NG, t=KT)

    xraw = sb("xraw", [P, 2, KT, S])
    xs = sb("xs", [P, 2, 2, KT, S], F32R)
    rope_t = sb("rope_t", [P, 2, 2, 1, DH])
    mask_t = sb("mask_t", [P, S])
    id_t = sb("id_t", [P, P])
    ones = sb("ones", [P, 32])
    rot1 = sb("rot1", [P, 2, BANK])
    rot2 = sb("rot2", [P, 2, BANK])
    qn = sb("qn", [P, NU, BANK])
    kx = sb("kx", [P, NU, NI, P])
    v_t = sb("v_t", [P, 2, KV])
    qt = sb("qt", [P, NU, 2, BANK], F32R)
    kt = sb("kt", [P, NU, 2, BANK], F32R)
    sm = sb("sm", [P, 2, BANK])
    smin = sb("smin", [P, 2, NI])
    pexp = sb("pexp", [P, 2, BANK])
    psum_row = sb("psum_row", [P, 2, NI])
    prec = sb("prec", [P, 2, NI])
    pn = sb("pn", [P, 2, BANK])
    pt = sb("pt", [P, NU, NI, NJ, S])
    ot = sb("ot", [P, NU, BANK])
    ctx_t = sb("ctx_t", [P, D])
    sq = sb("sq", [P, D])
    nb = sb("nb", [P, D])
    csum = sb("csum", [P, BANK])

    qkv_ps = [ps(f"qkv_ps{g}") for g in range(NG)]
    s_ps = ps("s_ps")
    turn_ps = ps("turn_ps")
    pt_ps = [ps("pt_ps0"), ps("pt_ps1")]
    o_ps = ps("o_ps")

    consts_in = sem("consts_in")
    w_in = [sem(f"w_in{n}") for n in range(4)]
    w_hi = sem("w_hi")
    w_lo = sem("w_lo")
    set_up = sem("set_up")
    x_in = [sem("x_in0"), sem("x_in1")]
    c_in = sem("c_in")
    x_hi = sem("x_hi")
    x_lo = sem("x_lo")
    qkv_done = sem("qkv_done")
    rope_read = sem("rope_read")
    roped = sem("roped")
    kx_turned = sem("kx_turned")
    kt_hi = sem("kt_hi")
    kt_lo = sem("kt_lo")
    q_turned = sem("q_turned")
    qt_hi = sem("qt_hi")
    qt_lo = sem("qt_lo")
    scored = sem("scored")
    masked = sem("masked")
    expd = sem("expd")
    inverted = sem("inverted")
    scaled = sem("scaled")
    p_turned = sem("p_turned")
    pt_read = sem("pt_read")
    pv_done = sem("pv_done")
    ot_read = sem("ot_read")
    ot_out = [sem("ot_out0"), sem("ot_out1")]
    sq_done = sem("sq_done")
    nb_done = sem("nb_done")
    summed = sem("summed")
    cs_read = sem("cs_read")
    cs_out = sem("cs_out")
    held = sem("held")
    later_in = [sem(f"later_in{n}") for n in range(4)]
    later_hi = sem("later_hi")
    later_lo = [sem("later_lo_dve"), sem("later_lo_pool")]
    cs_in = sem("cs_in")
    cs_edge = sem("cs_edge")
    root = sem("root")
    cos_step = sem("cos_step")
    sim_made = sem("sim_made")
    sim_out = sem("sim_out")

    LAST = B + 1
    LEAD, TAIL = 4, 4
    PERIOD = SLOTS // NC
    TURN = 2 * PERIOD + 1
    BEHIND = TURN // PERIOD
    STAGES = 4
    WK = 2
    GP = KT // WK
    PIECES = NG * GP
    HD = D // 2

    block = ctx.enter_context(nc.Block())

    def stage(n):
        u, i = divmod(n % STAGES, NI // WK)
        return pt[:, u, i * WK:(i + 1) * WK].rearrange("p i j s -> p i (j s)")

    def w_piece(n, part):
        return w_sb[:, part, n // GP, (n % GP) * WK:(n % GP + 1) * WK, :]

    wo_sb, wa_sb, wb_sb, wx_sb, sel_sb = later_weights(weights)
    LATER = KT + 3
    HA = KT // 2 * LOWW
    landing = [xraw[:, 0].rearrange("p t s -> p (t s)"), xraw[:, 1].rearrange("p t s -> p (t s)"), ctx_t[:], sq[:]]

    def later_parts(n):
        raw = landing[n % STAGES]
        if n < KT:
            return [(raw, wo_sb[:, 0, n], wo_sb[:, 1, n])]
        if n == KT + 2:
            return [(raw, wb_sb[:, 0], wb_sb[:, 1])]
        k = slice((n - KT) * KT // 2, (n - KT + 1) * KT // 2)
        half = (raw[:, 0:HA].rearrange("p (t n) -> p t n", n=LOWW), wa_sb[:, k, 0], wa_sb[:, k, 1])
        rest = raw[:, HA:HA + TAPS * P]
        return [half, (rest, wx_sb[:, 0], wx_sb[:, 1]) if n == KT else (rest, sel_sb, None)]

    def by_pool(n):
        return n % 3 == 1

    def later_done(eng, n):
        same = [m for m in range(n + 1) if by_pool(m) == by_pool(n)]
        wait(eng, later_lo[by_pool(n)], len(same))

    QD = D // 4
    sqs, nbs, norm = nb[:, 0:QD + 1], nb[:, QD + 1:2 * QD + 1], nb[:, 2 * QD + 1:3 * QD + 2]
    value = csum[:].rearrange("p (m n) -> p m n", m=2)
    simparts = xs[:, 0, 0].rearrange("p t s -> p (t s)").rearrange("p (m l n) -> p m l n", m=2, l=2)

    @block.sync
    def _(sp):
        def load_x(t, par):
            wait(sp, x_lo, after(t - 2, 2, 2))
            sp.dma_start(xraw[:, par], xT[t]).then_inc(x_in[par], 16)

        def load_ctx(t):
            wait(sp, sq_done, after(t - 1, 1, 1))
            wait(sp, nb_done, after(t - 1, 2, 2))
            sp.dma_start(ctx_t[:], ctx_in[t]).then_inc(c_in, 16)

        def load_later(n):
            if n < 2:
                wait(sp, x_lo, 2 * B)
            elif n == 2:
                wait(sp, sq_done, B)
                wait(sp, nb_done, 2 * B)
            elif n == 3:
                wait(sp, summed, B)
            else:
                later_done(sp, n - STAGES)
            raw, arrived = landing[n % STAGES], later_in[n % STAGES]
            if n < KT:
                sp.dma_start(raw, wo[:, n, :]).then_inc(arrived, 16)
            elif n == KT + 2:
                sp.dma_start(raw, wb).then_inc(arrived, 16)
            else:
                sp.dma_start(raw[:, 0:HA], wa[:, (n - KT) * HA:(n - KT + 1) * HA]).then_inc(arrived, 16)
                sp.dma_start(raw[:, HA:HA + TAPS * P], wx if n == KT else tapsel).then_inc(arrived, 16)

        def load_sums():
            sums = cs_dram.rearrange("b q n -> b (q n)")
            sp.wait_ge(cs_out, 16 * B)
            sp.wait_ge(summed, B)
            sp.wait_ge(cs_edge, 1)
            for q in range(4):
                rows, width = slice(q * B, (q + 1) * B), QD + 1 if q < 3 else QD
                sp.dma_start(sqs[rows, 0:width], sums[:, q * QD:q * QD + width]).then_inc(cs_in, 16)
                sp.dma_start(nbs[rows], sums[:, D + q * QD:D + (q + 1) * QD]).then_inc(cs_in, 16)

        def store_sims():
            sp.wait_ge(sim_made, 2)
            for q in range(4):
                sp.dma_start(sim_dram[:, :, q * QD:(q + 1) * QD],
                             simparts[q * B:(q + 1) * B].bitcast(F32).rearrange("p m l n -> p (m l) n")).then_inc(sim_out, 16)
            sp.wait_ge(sim_out, 16 * 4)

        sp.dma_start(xraw[:, 0], xT[0]).then_inc(x_in[0], 16)
        for n in range(PIECES):
            wait(sp, w_lo, n - STAGES + 1)
            sp.dma_start(stage(n), wqkv[n // GP, :, (n % GP) * WK:(n % GP + 1) * WK, :]).then_inc(w_in[n % STAGES], 16)
            if n == STAGES - 1:
                sp.dma_start(rope_t[:], rope).then_inc(consts_in, 16)
                sp.dma_start(mask_t[:], mask).then_inc(consts_in, 16)
                sp.dma_start(id_t[:], ident).then_inc(consts_in, 16)
                load_ctx(0)

        def step(t, par):
            a, b = t - 1, t - 2
            if valid(t + 1):
                load_x(t + 1, 1 - par)
                load_ctx(t + 1)
            if valid(b):
                wait(sp, ot_read, after(b, NU, 2))
                sp.dma_start(ot_dram[b, :, BANK:D], ot[:, 1]).then_inc(ot_out[1], 16)
            if valid(t):
                wait(sp, cs_read, after(t, 1, 1))
                sp.dma_start(cs_dram[t], csum[0:P:32, :]).then_inc(cs_out, 16)
            if isinstance(t, int) and t == B - 1:
                for n in range(STAGES):
                    load_later(n)
            if isinstance(t, int) and t == B:
                load_sums()
                for n in range(STAGES, LATER - 3):
                    load_later(n)
            if valid(a):
                wait(sp, ot_read, after(a, NU, 1))
                sp.dma_start(ot_dram[a, :, 0:BANK], ot[:, 0]).then_inc(ot_out[0], 16)
            if isinstance(t, int) and t == B:
                for n in range(LATER - 3, LATER):
                    load_later(n)

        steps(sp, step, 0, LAST, LEAD, TAIL)
        store_sims()
        for u in range(NU):
            sp.wait_ge(ot_out[u], 16 * B)

    @block.tensor
    def _(pe):
        def project(t, par, g, k):
            if g == 0 and k == 0:
                wait(pe, x_lo, after(t, 2, 2))
            if k == 0:
                wait(pe, rope_read, after(t - 1, NG, g + 1))
            if isinstance(t, int) and t == 0 and k % WK == 0:
                pe.wait_ge(w_lo, g * GP + k // WK + 1)
            for n, (xl, wl) in enumerate(((0, 0), (0, 1), (1, 0))):
                mm = pe.matmul(qkv_ps[g][:], xs[:, par, xl, k], w_sb[:, wl, g, k],
                               start=(k == 0 and n == 0), stop=(k == KT - 1 and n == 2))
            if k == KT - 1:
                mm.then_inc(qkv_done, 1)

        def turn_k(t, u):
            wait(pe, roped, after(t, NG, 1))
            if u == 0:
                wait(pe, qt_lo, after(t - 1, NU, NU))
            else:
                wait(pe, qt_lo, after(t, NU, 1))
            for i in range(NI):
                mm = pe.transpose(turn_ps[:, i * P:(i + 1) * P], kx[:, u, i], id_t[:])
            mm.then_inc(kx_turned, 1)

        def turn_q(t, u):
            wait(pe, roped, after(t, NG, 2 + u))
            if u == 0:
                wait(pe, cs_read, after(t, 1, 1))
            else:
                wait(pe, kt_lo, after(t, NU, NU))
            for j in range(NJ):
                mm = pe.transpose(turn_ps[:, j * P:(j + 1) * P], qn[:, u, j * P:(j + 1) * P], id_t[:])
            mm.then_inc(q_turned, 1)

        def score(a, c):
            u, j = divmod(c, NJ)
            wait(pe, qt_lo, after(a, NU, u + 1))
            wait(pe, kt_lo, after(a, NU, u + 1))
            wait(pe, masked, after(a, NC, c))
            for n, (ql, kl) in enumerate(((0, 0), (0, 1), (1, 0))):
                mm = pe.matmul(s_ps[:], qt[:, u, ql, j * P:(j + 1) * P], kt[:, u, kl],
                               start=(n == 0), stop=(n == 2))
            mm.then_inc(scored, 1)

        def turn_p(a, c):
            wait(pe, scaled, after(a, NC, c + 1))
            wait(pe, pt_read, after(a, NC, c - 1))
            for i in range(NI):
                mm = pe.transpose(pt_ps[c % 2][:, i * P:(i + 1) * P], pn[:, c % 2, i * P:(i + 1) * P], id_t[:])
            mm.then_inc(p_turned, 1)

        def weigh(a, par, u):
            wait(pe, pt_read, after(a, NC, NJ * (u + 1)))
            wait(pe, ot_read, after(a, NU, u))
            for i in range(NI):
                g = NI * u + i
                mm = pe.matmul(o_ps[32 * i:32 * i + 32, :], v_t[:, par, g * DH:(g + 1) * DH],
                               pt[:, u, i].rearrange("p j s -> p (j s)"), start=True, stop=True,
                               tile_position=(0, 32 * i))
            mm.then_inc(pv_done, 1)

        def sum_ctx(t):
            wait(pe, sq_done, after(t, 1, 1))
            wait(pe, nb_done, after(t, 2, 2))
            wait(pe, kt_lo, after(t, NU, 1))
            for m in range(4):
                src = (sq, nb)[m // 2]
                mm = pe.matmul(turn_ps[32 * m:32 * m + 32, :], ones[:], src[:, (m % 2) * BANK:(m % 2 + 1) * BANK],
                               start=True, stop=True, tile_position=(0, 32 * m))
            mm.then_inc(summed, 1)

        pe.wait_ge(consts_in, 48)
        pe.wait_ge(set_up, 3)

        def step(t, par):
            a, b = t - 1, t - 2
            for s in range(SLOTS):
                c = (s - TURN) // PERIOD
                if valid(a) and s % PERIOD == 0:
                    score(a, s // PERIOD)
                if s % PERIOD == TURN % PERIOD:
                    if c >= 0 and valid(a):
                        turn_p(a, c)
                    if c < 0 and valid(b):
                        turn_p(b, c + NC)
                if valid(a):
                    if s == 2:
                        turn_k(a, 1)
                    if s == 8:
                        turn_q(a, 1)
                    if s == 18:
                        weigh(a, 1 - par, 0)
                if valid(b) and s == 7:
                    weigh(b, par, 1)
                if valid(t):
                    if s == 11:
                        turn_k(t, 0)
                    if s == 14:
                        sum_ctx(t)
                    if s == 20:
                        turn_q(t, 0)
                    project(t, par, s // KT, s % KT)

        steps(pe, step, 0, LAST, LEAD, TAIL)

    @block.vector
    def _(dve):
        dve.memset(ones[:], 1.0).then_inc(set_up, 1)
        for n in range(PIECES):
            dve.wait_ge(w_hi, n + 1)
            dve.tensor_tensor(w_piece(n, 1), stage(n), w_piece(n, 0).bitcast(F32), ALU.subtract).then_inc(w_lo, 1)

        def rotate(t, par, g):
            r = (par + g) % 2
            src, width = qkv_ps[g], KV if g == 0 else BANK
            tab = rope_t[:, 1 if g == 0 else 0]
            heads = width // DH
            wait(dve, qkv_done, after(t, NG, g + 1))
            wait(dve, roped, after(t, NG, g - 1))
            q3 = src[:, 0:width].rearrange("p (h d) -> p h d", d=DH)
            o1 = rot1[:, r, 0:width].rearrange("p (h d) -> p h d", d=DH)
            o2 = rot2[:, r, 0:width].rearrange("p (h d) -> p h d", d=DH)
            cos = tab[:, 0, 0].unsqueeze(1).broadcast_to([P, heads, DH])
            dve.tensor_tensor(o1, q3, cos, ALU.mult)
            for z in range(2):
                sin = tab[:, 1, 0, z * HALF:(z + 1) * HALF].unsqueeze(1).broadcast_to([P, heads, HALF])
                ins = dve.tensor_tensor(o2[:, :, z * HALF:(z + 1) * HALF],
                                        q3[:, :, (1 - z) * HALF:(2 - z) * HALF], sin, ALU.mult)
            if g == 0:
                wait(dve, pv_done, after(t - 2, NU, NU))
                ins = dve.tensor_copy(v_t[:, par], src[:, KV:2 * KV])
            ins.then_inc(rope_read, 1)

        def low_q(t, u):
            wait(dve, qt_hi, after(t, NU, u + 1))
            dve.tensor_tensor(qt[:, u, 1], turn_ps[:], qt[:, u, 0].bitcast(F32), ALU.subtract).then_inc(qt_lo, 1)

        def low_k(t, u):
            wait(dve, kt_hi, after(t, NU, u + 1))
            dve.tensor_tensor(kt[:, u, 1], turn_ps[:], kt[:, u, 0].bitcast(F32), ALU.subtract).then_inc(kt_lo, 1)

        def mask_min(a, c):
            wait(dve, scored, after(a, NC, c + 1))
            wait(dve, expd, after(a, NC, c - 1))
            dve.sem_inc(held)
            for i in range(NI):
                ins = dve.tensor_tensor_reduce(sm[:, c % 2, i * P:(i + 1) * P], s_ps[:, i * P:(i + 1) * P],
                                               mask_t[:], 1.0, 3e38, ALU.add, ALU.min, smin[:, c % 2, i:i + 1])
            ins.then_inc(masked, 1)

        def invert(a, c):
            wait(dve, expd, after(a, NC, c + 1))
            wait(dve, scaled, after(a, NC, c - 1))
            dve.reciprocal(prec[:, c % 2], psum_row[:, c % 2]).then_inc(inverted, 1)

        def read_pt(a, c):
            u, j = divmod(c, NJ)
            wait(dve, p_turned, after(a, NC, c + 1))
            wait(dve, pv_done, after(a - 1, NU, u + 1))
            dve.tensor_copy(pt[:, u, :, j], pt_ps[c % 2][:].rearrange("p (i s) -> p i s", i=NI)).then_inc(pt_read, 1)

        def low_later(n):
            dve.wait_ge(later_hi, n + 1)
            for raw, hi, lo in later_parts(n):
                if lo is not None:
                    ins = dve.tensor_tensor(lo, raw, hi.bitcast(F32), ALU.subtract)
            ins.then_inc(later_lo[0], 1)

        def cosine():
            done = 0

            def chained(ins):
                nonlocal done
                ins.then_inc(cos_step, 1)
                done += 1
                dve.wait_ge(cos_step, done)

            dve.wait_ge(root, 1)
            dve.wait_ge(qkv_done, NG * B)
            chained(dve.tensor_scalar(norm, norm, COS_EPS, None, ALU.max))
            for m in range(2):
                chained(dve.tensor_tensor(value[:, m], norm[:, 0:QD], norm[:, m:QD + m], ALU.mult))
                chained(dve.reciprocal(value[:, m], value[:, m]))
                chained(dve.tensor_tensor(value[:, m], value[:, m], (sqs[:, 0:QD], nbs)[m], ALU.mult))
                chained(dve.tensor_copy(simparts[:, m, 0], value[:, m]))
                dve.tensor_tensor(simparts[:, m, 1], value[:, m], simparts[:, m, 0].bitcast(F32),
                                  ALU.subtract).then_inc(sim_made, 1)

        dve.wait_ge(consts_in, 48)

        def step(t, par):
            a, b = t - 1, t - 2
            for p in range(NC):
                if p > 0 and valid(a):
                    invert(a, p - 1)
                if p == 0 and valid(b):
                    invert(b, NC - 1)
                if p == 3 and valid(a):
                    low_q(a, 1)
                if p == 4 and valid(t):
                    low_k(t, 0)
                if p == 7 and valid(t):
                    low_q(t, 0)
                if valid(a):
                    mask_min(a, p)
                if p < BEHIND and valid(b):
                    read_pt(b, NC - BEHIND + p)
                if p >= BEHIND and valid(a):
                    read_pt(a, p - BEHIND)
                if p == 0 and valid(a):
                    rotate(a, 1 - par, 2)
                if p == 1 and valid(a):
                    low_k(a, 1)
                if p == 2 and valid(t):
                    rotate(t, par, 0)
                if p == 5 and valid(t):
                    rotate(t, par, 1)
                if isinstance(t, int) and t == B and not by_pool(p):
                    if p == 0:
                        dve.wait_ge(summed, B)
                        dve.memset(sqs[3 * B:P, QD:QD + 1], 0.0).then_inc(cs_edge, 1)
                    low_later(p)
            if isinstance(t, int) and t == B:
                for n in range(NC, LATER):
                    if not by_pool(n):
                        low_later(n)
            if isinstance(t, int) and t == LAST:
                cosine()

        steps(dve, step, 0, LAST, LEAD, TAIL)

    @block.scalar
    def _(act):
        def high_x(t, par):
            wait(act, x_in[par], arrivals(t, par))
            wait(act, qkv_done, after(t - 2, NG, NG))
            nc.scalar.copy(xs[:, par, 0], xraw[:, par]).then_inc(x_hi, 1)

        def square(t):
            wait(act, c_in, after(t, 16, 16))
            wait(act, summed, after(t - 1, 1, 1))
            nc.scalar.activation(sq[:], ctx_t[:], ACT.Square).then_inc(sq_done, 1)

        def high_q(t, u):
            wait(act, q_turned, after(t, NU, u + 1))
            wait(act, scored, after(t - 1, NC, NJ * (u + 1)))
            nc.scalar.copy(qt[:, u, 0], turn_ps[:]).then_inc(qt_hi, 1)

        def high_k(t, u):
            wait(act, kx_turned, after(t, NU, u + 1))
            wait(act, scored, after(t - 1, NC, NJ * (u + 1)))
            nc.scalar.copy(kt[:, u, 0], turn_ps[:]).then_inc(kt_hi, 1)

        def exponent(a, c):
            wait(act, masked, after(a, NC, c + 1))
            wait(act, scaled, after(a, NC, c - 1))
            wait(act, inverted, after(a, NC, c - 1))
            for i in range(NI):
                ins = nc.scalar.activation(pexp[:, c % 2, i * P:(i + 1) * P], sm[:, c % 2, i * P:(i + 1) * P],
                                           ACT.Exp, bias=smin[:, c % 2, i:i + 1], scale=-1.0,
                                           accum_out=psum_row[:, c % 2, i:i + 1])
            ins.then_inc(expd, 1)

        def read_ot(a, u):
            wait(act, pv_done, after(a, NU, u + 1))
            wait(act, ot_out[u], after(a, 16, 0))
            nc.scalar.copy(ot[:, u], o_ps[:]).then_inc(ot_read, 1)

        def read_sums(t):
            wait(act, summed, after(t, 1, 1))
            wait(act, cs_out, after(t, 16, 0))
            nc.scalar.copy(csum[:], turn_ps[:]).then_inc(cs_read, 1)

        def high_later(n):
            if n == 0:
                act.wait_ge(qkv_done, NG * B)
            parts = later_parts(n)
            act.wait_ge(later_in[n % STAGES], 16 * sum(len(later_parts(m)) for m in range(n % STAGES, n + 1, STAGES)))
            for raw, hi, _ in parts:
                ins = nc.scalar.copy(hi, raw)
            ins.then_inc(later_hi, 1)

        high_x(0, 0)
        for n in range(PIECES):
            act.wait_ge(w_in[n % STAGES], 16 * (n // STAGES + 1))
            nc.scalar.copy(w_piece(n, 0), stage(n)).then_inc(w_hi, 1)
            if n == PIECES // 2:
                square(0)

        def step(t, par):
            a, b = t - 1, t - 2
            for p in range(NC):
                if p == 1 and valid(a):
                    high_k(a, 1)
                if p == 2 and valid(t + 1):
                    high_x(t + 1, 1 - par)
                if p == 3 and valid(a):
                    high_q(a, 1)
                if p == 3 and valid(b):
                    read_ot(b, 1)
                if p == 4 and valid(t):
                    high_k(t, 0)
                if p == 5 and valid(t):
                    read_sums(t)
                if p == 6 and valid(t + 1):
                    square(t + 1)
                if p == 7 and valid(t):
                    high_q(t, 0)
                if p == 7 and valid(a):
                    read_ot(a, 0)
                if valid(a):
                    exponent(a, p)
                if isinstance(t, int) and t == B:
                    high_later(p)
            if isinstance(t, int) and t == B:
                for n in range(NC, LATER):
                    high_later(n)
                act.wait_ge(cs_in, 16 * 8)
                nc.scalar.activation(norm, sqs, ACT.Sqrt).then_inc(root, 1)

        steps(act, step, 0, LAST, LEAD, TAIL)

    @block.gpsimd
    def _(pool):
        def low_x(t, par, half):
            k = slice(half * KT // 2, (half + 1) * KT // 2)
            wait(pool, x_hi, after(t, 1, 1))
            pool.tensor_tensor(xs[:, par, 1, k], xraw[:, par, k], xs[:, par, 0, k].bitcast(F32),
                               ALU.subtract).then_inc(x_lo, 1)

        def neighbour(t, half):
            lo, hi = half * HD, min((half + 1) * HD, D - 1)
            wait(pool, c_in, after(t, 16, 16))
            wait(pool, summed, after(t - 1, 1, 1))
            pool.tensor_tensor(nb[:, lo:hi], ctx_t[:, lo:hi], ctx_t[:, lo + 1:hi + 1], ALU.mult).then_inc(nb_done, 1)

        def add_rope(t, par, g):
            r = (par + g) % 2
            width = KV if g == 0 else BANK
            wait(pool, rope_read, after(t, NG, g + 1))
            if g == 0:
                wait(pool, kx_turned, after(t - 1, NU, NU))
                for u in range(NU):
                    dst = diagonal(kx[:, u].rearrange("p i c -> p (i c)"))
                    cols = slice(u * P, (u + 1) * P)
                    ins = pool.tensor_tensor(dst, rot1[:, r, cols].rearrange("p (i d) -> p i d", d=DH),
                                             rot2[:, r, cols].rearrange("p (i d) -> p i d", d=DH), ALU.add)
            else:
                wait(pool, q_turned, after(t - 1, NU, g))
                ins = pool.tensor_tensor(qn[:, g - 1], rot1[:, r], rot2[:, r], ALU.add)
            ins.then_inc(roped, 1)

        def scale(a, c):
            wait(pool, inverted, after(a, NC, c + 1))
            wait(pool, p_turned, after(a, NC, c - 1))
            pool.tensor_tensor(pn[:, c % 2].rearrange("p (i s) -> p i s", i=NI),
                               pexp[:, c % 2].rearrange("p (i s) -> p i s", i=NI),
                               prec[:, c % 2].unsqueeze(2).broadcast_to([P, NI, S]), ALU.mult).then_inc(scaled, 1)

        pool.memset(kx[:], 0.0).then_inc(set_up, 1)
        pool.memset(nb[:, D - 1:D], 0.0).then_inc(set_up, 1)
        low_x(0, 0, 0)
        low_x(0, 0, 1)
        neighbour(0, 0)
        neighbour(0, 1)
        pool.wait_ge(set_up, 3)

        def low_later(n):
            pool.wait_ge(later_hi, n + 1)
            for raw, hi, lo in later_parts(n):
                if lo is not None:
                    ins = pool.tensor_tensor(lo, raw, hi.bitcast(F32), ALU.subtract)
            ins.then_inc(later_lo[1], 1)

        def step(t, par):
            a, b = t - 1, t - 2
            for p in range(NC):
                if p == 3 and valid(t):
                    add_rope(t, par, 0)
                if p == 6 and valid(t):
                    add_rope(t, par, 1)
                if p == 0 and valid(b):
                    scale(b, NC - 1)
                if p > 0 and valid(a):
                    scale(a, p - 1)
                if p == 1 and valid(a):
                    add_rope(a, 1 - par, 2)
                if p in (2, 3) and valid(t + 1):
                    low_x(t + 1, 1 - par, p - 2)
                if p in (5, 7) and valid(t + 1):
                    neighbour(t + 1, (p - 5) // 2)
                if isinstance(t, int) and t == B and by_pool(p):
                    low_later(p)
            if isinstance(t, int) and t == B:
                for n in range(NC, LATER):
                    if by_pool(n):
                        low_later(n)

        steps(pool, step, 0, LAST, LEAD, TAIL)


def diagonal(blocks):
    return bass.AP(tensor=blocks.tensor, offset=blocks.offset,
                   ap=[list(blocks.ap[0]), [P + DH, NI], [1, DH]])


def part2(nc, ctx, weights, x, br, ident, ot_dram, sim_dram, out):
    def sb(name, shape, dt=F32):
        return ctx.enter_context(nc.sbuf_tensor(name, shape, dt))

    def ps(name):
        return ctx.enter_context(nc.psum_tensor(name, [P, BANK], F32))

    def sem(name):
        return ctx.enter_context(nc.semaphore(name))

    wo_sb, wa_sb, wb_sb, wx_sb, sel_sb = later_weights(weights)
    wx_sb = wx_sb.rearrange("p l (k o) -> p l k o", k=TAPS)
    sel_sb = sel_sb.rearrange("p (k c) -> p k c", k=TAPS)

    PB = 3
    oraw = sb("oraw", [P, 2, D])
    os_t = sb("os_t", [P, 2, 2, KT, S], F32R)
    xn = sb("xn", [P, 2, D])
    yz = sb("yz", [P, 2, D])
    y3 = sb("y3", [P, D])
    x1 = sb("x1", [P, 2, D + 2])
    sim = sb("sim", [P, 2, D], F32R)
    prod = sb("prod", [P, PB, BANK])
    prods = sb("prods", [P, PB, 2, BANK], F32R)
    late = sb("late", [P, 2, 2, D])
    xt = sb("xt", [P, 2, KT, S], F32R)
    br_t = sb("br_t", [P, H])
    id_t = sb("id2_t", [P, P])
    lowhi = sb("lowhi", [P, LOWW])
    low = sb("low", [P, LOWW])
    logit = sb("logit", [P, H])
    nmax = sb("nmax", [P, 1])
    gate = sb("gate", [P, H])
    gsum = sb("gsum", [P, 1])
    grec = sb("grec", [P, 1])
    gated = sb("gated", [P, HR])
    lt = sb("lt", [P, 2, S], F32R)
    power = sb("power", [P, 1])
    stats = [sb(f"stats{n}", [P, 2, 6]) for n in range(3)]
    mv = [sb(f"mv{n}", [P, 2]) for n in range(3)]
    var = [sb(f"var{n}", [P, 1]) for n in range(3)]
    rstd = [sb(f"rstd{n}", [P, 1]) for n in range(3)]
    nmean3 = sb("nmean3", [P, 1])
    shift3 = sb("shift3", [P, 1])

    x2, res = late[:, 0], late[:, 1]
    wo_ps = [ps("wo_ps0"), ps("wo_ps1")]
    att_ps = [ps("att_ps0"), ps("att_ps1")]
    conv_ps = [ps("conv_ps0"), ps("conv_ps1")]
    ffn_ps = [ps("ffn_ps0"), ps("ffn_ps1")]

    consts_in = sem("consts2_in")
    set_up = sem("set_up2")
    o_in = [sem("o_in0"), sem("o_in1")]
    xn_in = [sem("xn_in0"), sem("xn_in1")]
    sim_in = [sem("sim_in0"), sem("sim_in1")]
    o_hi = sem("o_hi")
    o_lo = sem("o_lo")
    wo_done = sem("wo_done")
    added = [sem(f"added{n}") for n in range(3)]
    counted = [sem(f"counted{n}") for n in range(3)]
    averaged = [sem(f"averaged{n}") for n in range(3)]
    var_done = [sem(f"var_done{n}") for n in range(3)]
    rstd_done = [sem(f"rstd_done{n}") for n in range(3)]
    normed = [sem(f"normed{n}") for n in range(3)]
    att_done = sem("att_done")
    prod_done = sem("prod_done")
    prod_hi = sem("prod_hi")
    prod_lo = sem("prod_lo")
    conv_done = sem("conv_done")
    x2_turned = sem("x2_turned")
    xt_hi = sem("xt_hi")
    xt_lo = sem("xt_lo")
    low_done = sem("low_done")
    low_step = sem("low_step")
    gate_in = sem("gate_in")
    gate_done = sem("gate_done")
    gated_done = sem("gated_done")
    low_turned = sem("low_turned")
    lt_hi = sem("lt_hi")
    lt_lo = sem("lt_lo")
    ffn_done = sem("ffn_done")
    held = sem("held2")
    shifted = sem("shifted")
    stored = [sem("stored0"), sem("stored1")]

    LAST = B + 2
    LEAD, TAIL = 6, 5
    UNITS = 2 * TAPS
    SLOTS2 = 2 * KT
    LOWCHAIN = 4

    block = ctx.enter_context(nc.Block())

    @block.sync
    def _(sp):
        def load_o(t, par):
            wait(sp, o_lo, after(t - 2, 2, 2))
            sp.dma_start(oraw[:, par], ot_dram[t]).then_inc(o_in[par], 16)
            wait(sp, added[0], after(t - 2, 2, 2))
            sp.dma_start(xn[:, par], x[t]).then_inc(xn_in[par], 16)

        def load_sim(t, par):
            wait(sp, att_done, after(t - 2, UNITS, UNITS))
            sp.dma_start(sim[0:4, par].bitcast(F32), sim_dram[t]).then_inc(sim_in[par], 16)
            sp.dma_start(sim[4:6, par, 1:D].bitcast(F32), sim_dram[t, 2:4, 0:D - 1]).then_inc(sim_in[par], 16)

        load_o(0, 0)
        sp.dma_start(id_t[:], ident).then_inc(consts_in, 16)
        sp.dma_start(br_t[:], br).then_inc(consts_in, 16)
        sp.wait_ge(set_up, 4)

        def step(t, par):
            if valid(t + 1):
                load_o(t + 1, 1 - par)
            if valid(t):
                load_sim(t, par)
            if valid(t - 3):
                wait(sp, normed[2], after(t - 3, 1, 1))
                sp.dma_start(out[t - 3], res[:, 1 - par]).then_inc(stored[1 - par], 16)

        steps(sp, step, 0, LAST, LEAD, TAIL)
        for par in range(2):
            sp.wait_ge(stored[par], 16 * B // 2)

    @block.tensor
    def _(pe):
        def project(t, par, n, k):
            if n == 0 and k == 0:
                wait(pe, o_lo, after(t, 2, 2))
            if k == 0:
                wait(pe, added[0], after(t - 1, 2, n + 1))
            for m, (ol, wl) in enumerate(((0, 0), (0, 1), (1, 0))):
                mm = pe.matmul(wo_ps[n][:], os_t[:, par, ol, k], wo_sb[:, wl, k, n * BANK:(n + 1) * BANK],
                               start=(k == 0 and m == 0), stop=(k == KT - 1 and m == 2))
            if k == KT - 1:
                mm.then_inc(wo_done, 1)

        def spread(t, par, m):
            h, k = divmod(m, TAPS)
            if m == 0:
                wait(pe, sim_in[par], 2 * arrivals(t, par))
            wait(pe, prod_done, after(t, UNITS, m - 1))
            pe.matmul(att_ps[m % 2][:], sel_sb[:, k], sim[:, par, h * BANK:(h + 1) * BANK],
                      start=True, stop=True).then_inc(att_done, 1)

        def convolve(t, m):
            h, k = divmod(m, TAPS)
            wait(pe, prod_lo, after(t, UNITS, m + 1))
            if k == 0:
                wait(pe, added[1], after(t - 1, 2, h + 1))
            for n, (wl, xl) in enumerate(((0, 0), (1, 0), (0, 1))):
                mm = pe.matmul(conv_ps[h][:], wx_sb[:, wl, k], prods[:, m % PB, xl],
                               start=(k == 0 and n == 0), stop=(k == TAPS - 1 and n == 2))
            mm.then_inc(conv_done, 1)

        def turn_x2(t, par, n):
            wait(pe, normed[1], after(t, 1, 1))
            wait(pe, added[2], after(t - 1, 2, n + 1))
            for k in range(NJ):
                c = (n * NJ + k) * P
                mm = pe.transpose(ffn_ps[n][:, k * P:(k + 1) * P], x2[:, par, c:c + P], id_t[:])
            mm.then_inc(x2_turned, 1)

        def reduce_rank(t):
            wait(pe, xt_lo, after(t, 2, 2))
            for k in range(KT):
                for xl in range(2):
                    mm = pe.matmul(ffn_ps[0][:, 0:2 * LOWW], xt[:, xl, k],
                                   wa_sb[:, k].rearrange("p l n -> p (l n)"),
                                   start=(k == 0 and xl == 0), stop=(k == KT - 1 and xl == 1))
            mm.then_inc(low_done, 1)

        def turn_low(t):
            wait(pe, gated_done, after(t, 1, 1))
            pe.transpose(ffn_ps[1][:, 0:S], gated[:], id_t[:]).then_inc(low_turned, 1)

        def expand(t):
            wait(pe, lt_lo, after(t, 1, 1))
            for n in range(2):
                for m, (ll, wl) in enumerate(((0, 0), (0, 1), (1, 0))):
                    mm = pe.matmul(ffn_ps[n][:], lt[:, ll], wb_sb[:, wl, n * BANK:(n + 1) * BANK],
                                   start=(m == 0), stop=(m == 2))
                mm.then_inc(ffn_done, 1)

        pe.wait_ge(consts_in, 32)
        pe.wait_ge(set_up, 4)

        def step(t, par):
            o, c, f, z = t, t - 1, t - 2, t - 3
            for s in range(SLOTS2):
                if valid(f) and s == 1:
                    convolve(f, UNITS - 1)
                if valid(c):
                    if s % 2 == 0 and 0 <= (s - 2) // 2 < UNITS:
                        spread(c, 1 - par, (s - 2) // 2)
                    if s % 2 == 1 and 0 <= (s - 7) // 2 < UNITS - 1:
                        convolve(c, (s - 7) // 2)
                if valid(z) and s == 2:
                    expand(z)
                if valid(f):
                    if s in (7, 8):
                        turn_x2(f, par, s - 7)
                    if s == 11:
                        reduce_rank(f)
                    if s == 15:
                        turn_low(f)
                if valid(o):
                    project(o, par, s // KT, s % KT)

        steps(pe, step, 0, LAST, LEAD, TAIL)

    @block.vector
    def _(dve):
        dve.memset(power[:], -0.5).then_inc(set_up, 1)
        dve.memset(x1[:, :, 0:1], 0.0).then_inc(set_up, 1)
        dve.memset(x1[:, :, D + 1:D + 2], 0.0).then_inc(set_up, 1)
        dve.memset(sim[:].bitcast(F32), 0.0).then_inc(set_up, 1)

        def add(t, par, n, half):
            cols = slice(half * BANK, (half + 1) * BANK)
            if n == 0:
                wait(dve, wo_done, after(t, 2, half + 1))
                if half == 0:
                    wait(dve, xn_in[par], arrivals(t, par))
                dst = yz[:, 0, cols]
                ins = dve.tensor_tensor(dst, wo_ps[half][:], xn[:, par, cols], ALU.add)
            elif n == 1:
                wait(dve, conv_done, after(t, UNITS, TAPS * (half + 1)))
                dst = yz[:, 1, cols]
                ins = dve.tensor_tensor(dst, conv_ps[half][:], x1[:, par, 1 + half * BANK:1 + (half + 1) * BANK], ALU.add)
            else:
                wait(dve, ffn_done, after(t, 2, half + 1))
                wait(dve, normed[2], after(t - 1, 1, 1))
                dst = y3[:, cols]
                ins = dve.scalar_tensor_tensor(dst, ffn_ps[half][:], FFN_SCALE, x2[:, par, cols], ALU.mult, ALU.add)
            ins.then_inc(added[n], 1)
            dve.wait_ge(added[n], after(t, 2, half + 1))
            dve.bn_stats(stats[n][:, half], dst).then_inc(counted[n], 1)

        def average(t, n):
            dve.wait_ge(counted[n], after(t, 2, 2))
            dve.sem_inc(held)
            dve.bn_aggr(mv[n][:], stats[n][:]).then_inc(averaged[n], 1)
            dve.wait_ge(averaged[n], after(t, 1, 1))
            if n == 2:
                dve.tensor_scalar(nmean3[:], mv[n][:, 0:1], -1.0, None, ALU.mult)
            dve.tensor_scalar(var[n][:], mv[n][:, 1:2], LN_EPS, None, ALU.add).then_inc(var_done[n], 1)

        def normalise(t, par, n):
            src = yz[:, n]
            dst = (x1[:, par, 1:D + 1], x2[:, par])[n]
            wait(dve, rstd_done[n], after(t, 1, 1))
            dve.tensor_scalar(dst, src, mv[n][:, 0:1], rstd[n][:], ALU.subtract, ALU.mult).then_inc(normed[n], 1)

        def multiply(t, par, m):
            h, k = divmod(m, TAPS)
            wait(dve, att_done, after(t, UNITS, m + 1))
            wait(dve, prod_lo, after(t, UNITS, m - PB + 1))
            if m == 0:
                dve.wait_ge(normed[0], after(t, 1, 1))
            dve.tensor_tensor(prod[:, m % PB], att_ps[m % 2][:],
                              x1[:, par, h * BANK + k:h * BANK + k + BANK], ALU.mult).then_inc(prod_done, 1)

        def low_x2(t, n):
            wait(dve, xt_hi, after(t, 2, n + 1))
            dst = xt[:, :, n * NJ:(n + 1) * NJ].rearrange("p l t s -> p l (t s)")
            dve.tensor_tensor(dst[:, 1], ffn_ps[n][:], dst[:, 0].bitcast(F32), ALU.subtract).then_inc(xt_lo, 1)

        def route(t):
            wait(dve, low_done, after(t, 1, 1))
            dve.tensor_copy(lowhi[:], ffn_ps[0][:, LOWW:2 * LOWW]).then_inc(low_step, 1)
            dve.wait_ge(low_step, after(t, LOWCHAIN, 1))
            dve.tensor_tensor(low[:], ffn_ps[0][:, 0:LOWW], lowhi[:], ALU.add).then_inc(low_step, 1)
            dve.wait_ge(low_step, after(t, LOWCHAIN, 2))
            dve.tensor_tensor(logit[:], low[:, HR:LOWW], br_t[:], ALU.add).then_inc(low_step, 1)
            dve.wait_ge(low_step, after(t, LOWCHAIN, 3))
            dve.tensor_reduce(nmax[:], logit[:], AX.X, ALU.max, negate=True).then_inc(gate_in, 1)

        def gate_low(t):
            wait(dve, gate_done, after(t, 1, 1))
            dve.reciprocal(grec[:], gsum[:]).then_inc(low_step, 1)
            dve.wait_ge(low_step, after(t, LOWCHAIN, 4))
            dve.scalar_tensor_tensor(gated[:].rearrange("p (h r) -> p h r", h=H),
                                     low[:, 0:HR].rearrange("p (h r) -> p h r", h=H), grec[:],
                                     gate[:].unsqueeze(2).broadcast_to([P, H, R]),
                                     ALU.mult, ALU.mult).then_inc(gated_done, 1)

        def low_lt(t):
            wait(dve, lt_hi, after(t, 1, 1))
            dve.tensor_tensor(lt[:, 1], ffn_ps[1][:, 0:S], lt[:, 0].bitcast(F32), ALU.subtract).then_inc(lt_lo, 1)

        dve.wait_ge(consts_in, 32)

        def step(t, par):
            c, f, z = t - 1, t - 2, t - 3
            if valid(c):
                add(c, 1 - par, 0, 1)
                average(c, 0)
            if valid(f):
                add(f, par, 1, 1)
                average(f, 1)
            if valid(c):
                normalise(c, 1 - par, 0)
                multiply(c, 1 - par, 0)
            if valid(z):
                add(z, 1 - par, 2, 0)
            if valid(f):
                normalise(f, par, 1)
            if valid(c):
                multiply(c, 1 - par, 1)
            if valid(z):
                add(z, 1 - par, 2, 1)
                average(z, 2)
            if valid(c):
                multiply(c, 1 - par, 2)
            if valid(f):
                low_x2(f, 0)
            if valid(t):
                add(t, par, 0, 0)
            if valid(f):
                low_x2(f, 1)
            if valid(c):
                multiply(c, 1 - par, 3)
                multiply(c, 1 - par, 4)
                add(c, 1 - par, 1, 0)
            if valid(f):
                route(f)
            if valid(c):
                multiply(c, 1 - par, 5)
            if valid(f):
                gate_low(f)
                low_lt(f)

        steps(dve, step, 0, LAST, LEAD, TAIL)

    @block.scalar
    def _(act):
        def high_o(t, par):
            wait(act, o_in[par], arrivals(t, par))
            wait(act, wo_done, after(t - 2, 2, 2))
            nc.scalar.copy(os_t[:, par, 0].rearrange("p t s -> p (t s)"), oraw[:, par]).then_inc(o_hi, 1)

        def high_prod(t, m):
            wait(act, prod_done, after(t, UNITS, m + 1))
            wait(act, conv_done, after(t, UNITS, m - PB + 1))
            nc.scalar.copy(prods[:, m % PB, 0], prod[:, m % PB]).then_inc(prod_hi, 1)

        def high_x2(t, n):
            wait(act, x2_turned, after(t, 2, n + 1))
            wait(act, low_done, after(t - 1, 1, 1))
            nc.scalar.copy(xt[:, 0, n * NJ:(n + 1) * NJ].rearrange("p t s -> p (t s)"),
                           ffn_ps[n][:]).then_inc(xt_hi, 1)

        def gates(t):
            wait(act, gate_in, after(t, 1, 1))
            wait(act, gated_done, after(t - 1, 1, 1))
            nc.scalar.activation(gate[:], logit[:], ACT.Exp, bias=nmax[:], accum_out=gsum[:]).then_inc(gate_done, 1)

        def high_lt(t):
            wait(act, low_turned, after(t, 1, 1))
            wait(act, ffn_done, after(t - 1, 2, 2))
            nc.scalar.copy(lt[:, 0], ffn_ps[1][:, 0:S]).then_inc(lt_hi, 1)

        def normalise3(t, par):
            wait(act, shifted, after(t, 1, 1))
            wait(act, stored[par], arrivals(t, par) - 16)
            nc.scalar.activation(res[:, par], y3[:], ACT.Identity, bias=shift3[:], scale=rstd[2][:]).then_inc(normed[2], 1)

        high_o(0, 0)

        def step(t, par):
            c, f, z = t - 1, t - 2, t - 3
            if valid(t + 1):
                high_o(t + 1, 1 - par)
            if valid(c):
                high_prod(c, 0)
                high_prod(c, 1)
                high_prod(c, 2)
            if valid(f):
                high_x2(f, 0)
            if valid(z):
                normalise3(z, 1 - par)
            if valid(f):
                high_x2(f, 1)
            if valid(c):
                high_prod(c, 3)
                high_prod(c, 4)
            if valid(f):
                gates(f)
            if valid(c):
                high_prod(c, 5)
            if valid(f):
                high_lt(f)

        steps(act, step, 0, LAST, LEAD, TAIL)

    @block.gpsimd
    def _(pool):
        def low_o(t, par, half):
            cols = slice(half * D // 2, (half + 1) * D // 2)
            wait(pool, o_hi, after(t, 1, 1))
            hi, lo = (os_t[:, par, part].rearrange("p t s -> p (t s)")[:, cols] for part in range(2))
            pool.tensor_tensor(lo, oraw[:, par, cols], hi.bitcast(F32), ALU.subtract).then_inc(o_lo, 1)

        def invert_root(t, n):
            wait(pool, var_done[n], after(t, 1, 1))
            wait(pool, normed[n], after(t - 1, 1, 1))
            pool.tensor_tensor(rstd[n][:], var[n][:], power[:], ALU.pow).then_inc(rstd_done[n], 1)
            if n == 2:
                pool.wait_ge(rstd_done[n], after(t, 1, 1))
                pool.tensor_tensor(shift3[:], nmean3[:], rstd[n][:], ALU.mult).then_inc(shifted, 1)

        def low_prod(t, m):
            wait(pool, prod_hi, after(t, UNITS, m + 1))
            pool.tensor_tensor(prods[:, m % PB, 1], prod[:, m % PB], prods[:, m % PB, 0].bitcast(F32),
                               ALU.subtract).then_inc(prod_lo, 1)

        low_o(0, 0, 0)
        low_o(0, 0, 1)
        pool.wait_ge(set_up, 4)

        def step(t, par):
            c, f, z = t - 1, t - 2, t - 3
            if valid(c):
                invert_root(c, 0)
            if valid(t + 1):
                low_o(t + 1, 1 - par, 0)
            if valid(f):
                invert_root(f, 1)
            if valid(c):
                low_prod(c, 0)
            if valid(t + 1):
                low_o(t + 1, 1 - par, 1)
            if valid(c):
                low_prod(c, 1)
            if valid(z):
                invert_root(z, 2)
            if valid(c):
                for m in range(2, UNITS):
                    low_prod(c, m)

        steps(pool, step, 0, LAST, LEAD, TAIL)


def rope_tables():
    inv = np.float32(1.0) / np.float32(10000.0) ** (np.arange(0, DH, 2, dtype=np.float32) / np.float32(DH))
    angle = np.arange(S, dtype=np.float32)[:, None] * inv[None, :].astype(np.float32)
    cos = np.concatenate([np.cos(angle)] * 2, axis=1)
    sin = np.concatenate([-np.sin(angle), np.sin(angle)], axis=1)
    scale = np.array([-float(DH) ** -0.5, 1.0])
    tab = scale[None, :, None, None] * np.stack([cos, sin], axis=1)[:, None]
    return np.ascontiguousarray(tab.astype(np.float32).reshape(S, 2, 2, 1, DH))


def tap_selectors():
    sel = np.zeros((P, TAPS, S), np.float32)
    first_row = {0: 4, 1: 0, 2: 2}
    for k in range(TAPS):
        for c in range(S):
            row = first_row[(TAPS * c + k) // S]
            sel[row:row + 2, k, c] = 1.0
    return sel.reshape(P, TAPS * S)


def kernel(**inputs):
    import concourse.bacc as bacc
    from concourse.bass_utils import run_bass_kernel_spmd

    f = {k: np.asarray(v) for k, v in inputs.items()}
    heads = (NU, NI, NJ, DH)
    q = f["L0_attn_wq"].reshape(*heads, D).transpose(0, 2, 1, 3, 4).reshape(D, D)
    cols = np.concatenate([f["L0_attn_wk"], f["L0_attn_wv"], q]).reshape(NG, BANK, KT, P)
    low = np.concatenate([f["L0_ffn_A"].reshape(HR, D), f["L0_ffn_Wr"]]).reshape(LOWW, KT, P)
    keys = np.arange(S)
    arrays = {
        "xT": f["x"].reshape(B, S, KT, P).transpose(0, 3, 2, 1),
        "x": f["x"],
        "ctx": f["ctx_4096"],
        "wqkv": cols.transpose(0, 3, 2, 1),
        "wo": f["L0_attn_wo"].reshape(D, *heads).transpose(2, 4, 1, 3, 0).reshape(P, KT, D),
        "wx": f["L0_xattn_weight"].transpose(1, 2, 0).reshape(S, TAPS * S),
        "wa": low.transpose(2, 1, 0).reshape(P, KT * LOWW),
        "wb": f["L0_ffn_B"].transpose(0, 2, 1).reshape(HR, D),
        "br": np.broadcast_to(f["L0_ffn_br"], (P, H)),
        "rope": rope_tables(),
        "mask": np.where(keys[None, :] > keys[:, None], np.float32(MASKED), np.float32(0.0)),
        "ident": np.eye(P, dtype=np.float32),
        "tapsel": tap_selectors(),
    }
    arrays = {f"in_{k}": np.ascontiguousarray(v) for k, v in arrays.items()}
    nc = bacc.Bacc("TRN2", target_bir_lowering=False, num_devices=1)
    args = [nc.dram_tensor(k, v.shape, mybir.dt.from_np(v.dtype), kind="ExternalInput").ap()
            for k, v in arrays.items()]
    out = nc.dram_tensor("out", (B, S, D), F32, kind="ExternalOutput").ap()
    build(nc, *args, out)
    r = run_bass_kernel_spmd(nc, [arrays], core_ids=[0])
    return r.results[0]["out"]
```

```python
from contextlib import ExitStack

import numpy as np

import concourse.bass as bass
from concourse import mybir

F32 = mybir.dt.float32
F32R = mybir.dt.float32r
ALU = mybir.AluOpType
ACT = mybir.ActivationFunctionType
AX = mybir.AxisListType

B, S, D = 32, 128, 1024
P = 128
KT = D // P
HEADS, KVH, DH = 32, 8, 32
NU = 2
NI = KVH // NU
NJ = HEADS // KVH
NC = NU * NJ
HALF = DH // 2
BANK = 512
KV = KVH * DH
NG = 3
SLOTS = NG * KT
R, H = 16, 8
HR = H * R
LOWW = HR + H
FFN_SCALE = float(H) * 2.0
LN_EPS = 1e-5
COS_EPS = 1e-8
MASKED = 1e30
TAPS = 3
CB = D // P
SIM_PAD = 16

SIM_TABLE = (0, 0, 1, 2, 2)
RUNS = [(-(-S * m // TAPS), S * (m + 1) // TAPS) for m in range(TAPS)]
EDGES = [RUNS[m][1] for m in range(TAPS - 1)]
assert [SIM_TABLE[2 * e + k] for e in range(2) for k in range(TAPS)] == \
    [(TAPS * c + k) // S for c in EDGES for k in range(TAPS)]


def after(t, per, k):
    return t * per + k


def arrivals(t, par):
    return (t - par) * (16 // 2) + 16


def wait(eng, sem, count):
    if isinstance(count, int) and count <= 0:
        return
    eng.wait_ge(sem, count)


def valid(t):
    return not isinstance(t, int) or 0 <= t < B


def at_step(t, n):
    return isinstance(t, int) and t == n


def steps(eng, step, first, last, lead, tail):
    lo, hi = first + lead, last - tail + 1
    assert lo % 2 == 0 and hi % 2 == 0
    for t in range(first, lo):
        step(t, t % 2)
    with eng.Fori(lo // 2, hi // 2) as i:
        step(i * 2, 0)
        step(i * 2 + 1, 1)
    for t in range(hi, last + 1):
        step(t, t % 2)


def later_weights(weights):
    hi, lo = (weights[:, part * NG * KT * BANK:(part + 1) * NG * KT * BANK] for part in range(2))
    both = weights[:].rearrange("p (l m) -> p l m", l=2)
    rest = KT * D + D
    return (both[:, :, 0:KT * D].rearrange("p l (t n) -> p l t n", t=KT),
            hi[:, rest:rest + KT * 2 * LOWW].rearrange("p (t l n) -> p t l n", t=KT, l=2),
            both[:, :, KT * D:rest],
            lo[:, rest:rest + 2 * TAPS * P].rearrange("p (l n) -> p l n", l=2))


def build(nc, xT, x, ctx_in, wqkv, wo, wx, wa, wb, br, rope, mask, ident, out):
    ot_dram = nc.dram_tensor("ot_scratch", [B, P, D], F32, kind="Internal").ap()
    cs_dram = nc.dram_tensor("cs_scratch", [B, 2, D], F32, kind="Internal").ap()
    sim_dram = nc.dram_tensor("sim_scratch", [B, len(SIM_TABLE), D + SIM_PAD], F32, kind="Internal").ap()
    with ExitStack() as both:
        weights = both.enter_context(nc.sbuf_tensor("weights", [P, 2 * NG * KT * BANK], F32R))
        raw = both.enter_context(nc.sbuf_tensor("raw", [P, 2, D], F32))
        halves = both.enter_context(nc.sbuf_tensor("halves", [P, 2, 2, KT, S], F32R))
        wo_ps = [both.enter_context(nc.psum_tensor(f"wo_ps{n}", [P, BANK], F32)) for n in range(2)]
        xn0 = both.enter_context(nc.sbuf_tensor("xn0", [P, D], F32))
        handoff = (
            xn0, [both.enter_context(nc.semaphore(f"xn_in{n}")) for n in range(2)],
            [both.enter_context(nc.semaphore(f"o_in{n}")) for n in range(2)],
            both.enter_context(nc.semaphore("o_hi")),
            both.enter_context(nc.semaphore("o_lo")),
            both.enter_context(nc.semaphore("wo_done")),
            [both.enter_context(nc.semaphore(f"ot_out{n}")) for n in range(NU)],
            both.enter_context(nc.semaphore("ot_read")),
            both.enter_context(nc.semaphore("sim_made")),
            both.enter_context(nc.semaphore("sim_out")),
            (raw[:, 0, 0:D // 4], raw[:, 0, D // 4:BANK], raw[:, 0, BANK:D]))
        with ExitStack() as ctx:
            part1(nc, ctx, weights, raw, halves, wo_ps, handoff, xT, ctx_in, wqkv, wo, wx, wa, wb,
                  rope, mask, ident, x, ot_dram, cs_dram, sim_dram)
        with ExitStack() as ctx:
            part2(nc, ctx, weights, raw, halves, wo_ps, handoff, x, br, ident, ot_dram, sim_dram, out)


def part1(nc, ctx, weights, raw, halves, wo_ps, handoff, xT, ctx_in, wqkv, wo, wx, wa, wb,
          rope, mask, ident, x, ot_dram, cs_dram, sim_dram):
    def sb(name, shape, dt=F32):
        return ctx.enter_context(nc.sbuf_tensor(name, shape, dt))

    def ps(name):
        return ctx.enter_context(nc.psum_tensor(name, [P, BANK], F32))

    def sem(name):
        return ctx.enter_context(nc.semaphore(name))

    w_sb = weights[:].rearrange("p (l g t n) -> p l g t n", l=2, g=NG, t=KT)

    xraw = raw[:].rearrange("p a (t s) -> p a t s", t=KT)
    xs = halves
    xn0, xn_in, o_in, o_hi, o_lo, wo_done, ot_out, ot_read, sim_made, sim_out, kept = handoff
    rope_t = sb("rope_t", [P, 2, 2, 1, DH])
    mask_t = sb("mask_t", [P, S])
    id_t = sb("id_t", [P, P])
    zero = sb("zero", [P, 1])
    rot1 = sb("rot1", [P, 2, BANK])
    rot2 = sb("rot2", [P, 2, BANK])
    qn = (sb("qn0", [P, D]), xn0)
    kx = sb("kx", [P, NU, NI, P])
    v_t = sb("v_t", [P, 2, KV])
    qt = sb("qt", [P, NU, D], F32R)
    kt = sb("kt", [P, NU, 2, BANK], F32R)
    sm = sb("sm", [P, 2, BANK])
    smin = sb("smin", [P, 2, NI])
    pexp = sb("pexp", [P, 2, BANK])
    psum_row = sb("psum_row", [P, 2, NI])
    prec = sb("prec", [P, 2, NI])
    pn = sb("pn", [P, 2, BANK])
    pt = sb("pt", [P, NU, NI, NJ, S])
    ot = sb("ot", [P, NU, BANK])
    ctx_t = sb("ctx_t", [P, (CB + 1) * S])
    sq = sb("sq", [P, D])
    nb = sb("nb", [P, D])
    csum = sb("csum", [P, 2, CB])

    qkv_ps = wo_ps + [ps("qkv_ps2")]
    s_ps = ps("s_ps")
    turn_ps = ps("turn_ps")
    pt_ps = [ps("pt_ps0"), ps("pt_ps1")]
    o_ps = ps("o_ps")

    consts_in = sem("consts_in")
    w_in = [sem(f"w_in{n}") for n in range(4)]
    w_hi = sem("w_hi")
    w_lo = sem("w_lo")
    set_up = sem("set_up")
    x_in = [sem("x_in0"), sem("x_in1")]
    c_in = sem("c_in")
    x_hi = sem("x_hi")
    x_lo = sem("x_lo")
    qkv_done = sem("qkv_done")
    rope_read = sem("rope_read")
    roped = sem("roped")
    kx_turned = sem("kx_turned")
    kt_hi = sem("kt_hi")
    kt_lo = sem("kt_lo")
    q_turned = sem("q_turned")
    qt_hi = sem("qt_hi")
    qt_lo = sem("qt_lo")
    scored = sem("scored")
    masked = sem("masked")
    expd = sem("expd")
    inverted = sem("inverted")
    scaled = sem("scaled")
    p_turned = sem("p_turned")
    pt_read = sem("pt_read")
    pv_done = sem("pv_done")
    sq_done = sem("sq_done")
    nb_done = sem("nb_done")
    summed = sem("summed")
    cs_out = sem("cs_out")
    held = sem("held")
    later_in = [sem(f"later_in{n}") for n in range(3)]
    later_hi = sem("later_hi")
    later_lo = [sem("later_lo_dve"), sem("later_lo_pool")]
    cs_in = sem("cs_in")
    cs_edge = sem("cs_edge")
    root = sem("root")
    cos_step = sem("cos_step")

    LAST = B + 1
    LEAD, TAIL = 4, 4
    PERIOD = SLOTS // NC
    ADDS = 1 + 2 * NU
    TURNS = 2 * NU
    ROWS = P // 2
    TURN = 2 * PERIOD + 1
    AHEAD = 4
    BEHIND = TURN // PERIOD
    STAGES = 4
    WK = 2
    GP = KT // WK
    PIECES = NG * GP
    HD = D // 2

    block = ctx.enter_context(nc.Block())

    def stage(n):
        u, i = divmod(n % STAGES, NI // WK)
        return pt[:, u, i * WK:(i + 1) * WK].rearrange("p i j s -> p i (j s)")

    def w_piece(n, part):
        return w_sb[:, part, n // GP, (n % GP) * WK:(n % GP + 1) * WK, :]

    wo_sb, wa_sb, wb_sb, wx_sb = later_weights(weights)
    LATER = KT + 3
    BY_POOL = (1, 4, 8, 9)
    HA = KT // 2 * LOWW
    landing = [raw[:, 1], ctx_t[:, 0:D], sq[:]]

    def lands(n):
        return n % 3 if n < KT + 1 else 2 - n % 2

    def later_parts(n):
        src = landing[lands(n)]
        if n < KT:
            return [(src, wo_sb[:, 0, n], wo_sb[:, 1, n])]
        if n == KT + 1:
            return [(src, wb_sb[:, 0], wb_sb[:, 1])]
        k = slice((n - KT) // 2 * KT // 2, ((n - KT) // 2 + 1) * KT // 2)
        half = (src[:, 0:HA].rearrange("p (t n) -> p t n", n=LOWW), wa_sb[:, k, 0], wa_sb[:, k, 1])
        return [half, (src[:, HA:HA + TAPS * P], wx_sb[:, 0], wx_sb[:, 1])] if n == KT else [half]

    def later_done(eng, n):
        by = n in BY_POOL
        wait(eng, later_lo[by], sum((m in BY_POOL) == by for m in range(n + 1)))

    QD = D // 4
    sqs, nbs, norm = nb[:, 0:QD + 1], nb[:, QD + 1:2 * QD + 1], nb[:, 2 * QD + 1:3 * QD + 2]
    own, right, ot_last = kept

    @block.sync
    def _(sp):
        def load_x(t, par):
            wait(sp, x_lo, after(t - 2, 2, 2))
            sp.dma_start(xraw[:, par], xT[t]).then_inc(x_in[par], 16)

        def load_ctx(t):
            wait(sp, sq_done, after(t - 1, 1, 1))
            wait(sp, nb_done, after(t - 1, 2, 2))
            first = ctx_in[t, 0, 0:1]
            sp.dma_start(ctx_t[:], bass.AP(tensor=first.tensor, offset=first.offset,
                                           ap=[[CB * S, P], [1, (CB + 1) * S]])).then_inc(c_in, 16)

        def load_later(n):
            if n == 0:
                wait(sp, x_lo, 2 * B)
            elif n == 1:
                wait(sp, sq_done, B)
                wait(sp, nb_done, 2 * B)
            elif n == 2:
                wait(sp, sq_done, B)
            else:
                later_done(sp, max(m for m in range(n) if lands(m) == lands(n)))
            dst, arrived = landing[lands(n)], later_in[lands(n)]
            if n < KT:
                sp.dma_start(dst, wo[:, n, :]).then_inc(arrived, 16)
            elif n == KT + 1:
                sp.dma_start(dst, wb).then_inc(arrived, 16)
            else:
                sp.dma_start(dst[:, 0:HA], wa[:, (n - KT) // 2 * HA:((n - KT) // 2 + 1) * HA]).then_inc(arrived, 16)
            if n == KT:
                sp.dma_start(dst[:, HA:HA + TAPS * P], wx).then_inc(arrived, 16)

        def load_o(t):
            wait(sp, x_lo, 2 * (B - 1 + t))
            if t == 1:
                later_done(sp, KT - 2)
            for u in range(NU):
                wait(sp, ot_out[u], after(t, 16, 16))
            sp.dma_start(raw[:, t], ot_dram[t]).then_inc(o_in[t], 16)

        def load_sums():
            sums = cs_dram[0, 0, 0:1]
            sp.wait_ge(cs_out, 16 * B)
            sp.wait_ge(summed, B)
            for dst, at, width in ((sqs, 0, QD + 1), (nbs, D, QD)):
                sp.dma_start(dst, bass.AP(tensor=sums.tensor, offset=sums.offset + at,
                                          ap=[[2 * D, B], [QD, 4], [1, width]])).then_inc(cs_in, 16)

        def store_zeros():
            sp.wait_ge(set_up, 2)
            for row in range(2):
                sp.dma_start(sim_dram[:, row, 0:1], zero[0:B, :],
                             allow_slow_non_contiguous=True).then_inc(sim_out, 16)

        def store_own():
            sp.wait_ge(sim_made, 1)
            sp.dma_start(sim_row(sim_dram, 2, 0), own).then_inc(sim_out, 16)

        sp.dma_start(xraw[:, 0], xT[0]).then_inc(x_in[0], 16)
        for n in range(PIECES):
            wait(sp, w_lo, n - STAGES + 1)
            sp.dma_start(stage(n), wqkv[n // GP, :, (n % GP) * WK:(n % GP + 1) * WK, :]).then_inc(w_in[n % STAGES], 16)
            if n == GP + 1:
                sp.dma_start(rope_t[:], rope).then_inc(consts_in, 16)
                sp.dma_start(mask_t[:], mask).then_inc(consts_in, 16)
                sp.dma_start(id_t[:], ident).then_inc(consts_in, 16)
        load_x(1, 1)
        load_ctx(0)
        store_zeros()

        def step(t, par):
            a, b = t - 1, t - 2
            if valid(t + 1):
                if not at_step(t, 0):
                    load_x(t + 1, 1 - par)
                load_ctx(t + 1)
            if at_step(t, B - 1):
                load_later(0)
                load_later(1)
                load_o(0)
            if at_step(t, B):
                load_sums()
                load_later(5)
                load_later(6)
            if at_step(t, LAST):
                store_own()
            if valid(b) and not at_step(b, B - 1):
                wait(sp, ot_read, after(b, NU, 2))
                sp.dma_start(ot_dram[b, :, BANK:D], ot[:, 1]).then_inc(ot_out[1], 16)
            if at_step(t, B):
                load_later(7)
                load_later(8)
                load_o(1)
                wait(sp, q_turned, TURNS * B)
                sp.dma_start(xn0[:], x[0]).then_inc(xn_in[0], 16)
                load_later(9)
            if valid(t):
                wait(sp, sq_done, after(t, 1, 1))
                wait(sp, summed, after(t, 1, 1))
                sums = cs_dram[t, 0, 0:1]
                sp.dma_start(bass.AP(tensor=sums.tensor, offset=sums.offset, ap=[[CB, P], [D, 2], [1, CB]]),
                             csum[:]).then_inc(cs_out, 16)
            if at_step(t, B - 1):
                load_later(2)
                load_later(3)
            if at_step(t, B):
                load_later(10)
            if valid(a):
                wait(sp, ot_read, after(a, NU, 1))
                sp.dma_start(ot_dram[a, :, 0:BANK], ot[:, 0]).then_inc(ot_out[0], 16)
            if at_step(t, B - 1):
                load_later(4)

        steps(sp, step, 0, LAST, LEAD, TAIL)
        sp.wait_ge(ot_out[0], 16 * B)
        sp.wait_ge(ot_out[1], 16 * (B - 1))

    @block.tensor
    def _(pe):
        def project(t, par, g, k):
            if g == 0 and k == 0:
                wait(pe, x_lo, after(t, 2, 2))
            if k == 0:
                wait(pe, rope_read, after(t - 1, NG, g + 1))
            if isinstance(t, int) and t == 0 and k % WK == 0:
                pe.wait_ge(w_lo, g * GP + k // WK + 1)
            for n, (xl, wl) in enumerate(((0, 0), (0, 1), (1, 0))):
                mm = pe.matmul(qkv_ps[g][:], xs[:, par, xl, k], w_sb[:, wl, g, k],
                               start=(k == 0 and n == 0), stop=(k == KT - 1 and n == 2))
            if k == KT - 1:
                mm.then_inc(qkv_done, 1)

        def turn_k(t, u):
            wait(pe, roped, after(t, ADDS, 1))
            if u == 0:
                wait(pe, qt_lo, after(t - 1, TURNS, TURNS))
            else:
                wait(pe, qt_lo, after(t, TURNS, 2))
            for i in range(NI):
                mm = pe.transpose(turn_ps[:, i * P:(i + 1) * P], kx[:, u, i], id_t[:])
            mm.then_inc(kx_turned, 1)

        def turn_q(t, u, half):
            wait(pe, roped, after(t, ADDS, 2 + 2 * u + half))
            if half == 1:
                wait(pe, qt_lo, after(t, TURNS, 2 * u + 1))
            elif u == 1:
                wait(pe, kt_lo, after(t, NU, NU))
            else:
                wait(pe, kt_lo, after(t, NU, 1))
            for n in range(NJ):
                tile = half * NJ + n
                mm = pe.transpose(turn_ps[:, n * P:(n + 1) * P], qn[u][:, tile * P:(tile + 1) * P], id_t[:])
            mm.then_inc(q_turned, 1)

        def score(a, c):
            u, j = divmod(c, NJ)
            wait(pe, qt_lo, after(a, TURNS, 2 * u + j // 2 + 1))
            wait(pe, kt_lo, after(a, NU, u + 1))
            wait(pe, masked, after(a, NC, c))
            for pair in range(2):
                tile, keys = 2 * j + pair, slice(pair * 2 * P, (pair + 1) * 2 * P)
                for part in range(2):
                    mm = pe.matmul(s_ps[:, keys], qt[:, u, tile * P:(tile + 1) * P], kt[:, u, part, keys],
                                   start=(part == 0), stop=(part == 1))
            mm.then_inc(scored, 1)

        def turn_p(a, c):
            wait(pe, scaled, after(a, NC, c + 1))
            wait(pe, pt_read, after(a, NC, c - 1))
            for i in range(NI):
                mm = pe.transpose(pt_ps[c % 2][:, i * P:(i + 1) * P], pn[:, c % 2, i * P:(i + 1) * P], id_t[:])
            mm.then_inc(p_turned, 1)

        def weigh(a, par, u):
            wait(pe, pt_read, after(a, NC, NJ * (u + 1)))
            wait(pe, ot_read, after(a, NU, u))
            for i in range(NI):
                g = NI * u + i
                mm = pe.matmul(o_ps[32 * i:32 * i + 32, :], v_t[:, par, g * DH:(g + 1) * DH],
                               pt[:, u, i].rearrange("p j s -> p (j s)"), start=True, stop=True,
                               tile_position=(0, 32 * i))
            mm.then_inc(pv_done, 1)

        def project_out(n, k):
            if n == 0 and k == 0:
                wait(pe, o_lo, 2)
            if n == 0:
                later_done(pe, k)
            if k == 0:
                wait(pe, rope_read, after(B - 1, NG, n + 1))
            for m, (ol, wl) in enumerate(((0, 0), (0, 1), (1, 0))):
                mm = pe.matmul(wo_ps[n][:], halves[:, 0, ol, k], wo_sb[:, wl, k, n * BANK:(n + 1) * BANK],
                               start=(k == 0 and m == 0), stop=(k == KT - 1 and m == 2))
            if k == KT - 1:
                mm.then_inc(wo_done, 1)

        def step(t, par):
            a, b = t - 1, t - 2
            if at_step(t, 0):
                for s in range(SLOTS):
                    if s == 2 * KT:
                        pe.wait_ge(consts_in, 48)
                        pe.wait_ge(set_up, 2)
                        turn_k(0, 0)
                    project(0, 0, s // KT, s % KT)
                turn_q(0, 0, 0)
                for k in range(AHEAD):
                    project(1, 1, 0, k)
                turn_q(0, 0, 1)
                return
            for s in range(SLOTS):
                c = (s - TURN) // PERIOD
                if valid(a) and s % PERIOD == 0:
                    score(a, s // PERIOD)
                if s % PERIOD == TURN % PERIOD:
                    if c >= 0 and valid(a):
                        turn_p(a, c)
                    if c < 0 and valid(b):
                        turn_p(b, c + NC)
                if valid(a):
                    if s == 2:
                        turn_k(a, 1)
                    if s in (6, 9):
                        turn_q(a, 1, (s - 6) // 3)
                    if s == 18:
                        weigh(a, 1 - par, 0)
                if valid(b) and s == 7:
                    weigh(b, par, 1)
                if valid(t):
                    if s == 12:
                        turn_k(t, 0)
                    if s in (20, 23):
                        turn_q(t, 0, (s - 20) // 3)
                    if not (at_step(t, 1) and s < AHEAD):
                        project(t, par, s // KT, s % KT)
                if at_step(t, B) and s % PERIOD > 0:
                    project_out(s % PERIOD - 1, s // PERIOD)

        steps(pe, step, 0, LAST, LEAD, TAIL)

    @block.vector
    def _(dve):
        def rotate(t, par, g):
            r = (par + g) % 2
            src, width = qkv_ps[g], KV if g == 0 else BANK
            tab = rope_t[:, 1 if g == 0 else 0]
            heads = width // DH
            wait(dve, qkv_done, after(t, NG, g + 1))
            added = after(t, ADDS, 1) if g == 2 else after(t - 1, ADDS, 3 + 2 * g)
            wait(dve, roped, added)
            q3 = src[:, 0:width].rearrange("p (h d) -> p h d", d=DH)
            o1 = rot1[:, r, 0:width].rearrange("p (h d) -> p h d", d=DH)
            o2 = rot2[:, r, 0:width].rearrange("p (h d) -> p h d", d=DH)
            cos = tab[:, 0, 0].unsqueeze(1).broadcast_to([P, heads, DH])
            dve.tensor_tensor(o1, q3, cos, ALU.mult)
            for z in range(2):
                sin = tab[:, 1, 0, z * HALF:(z + 1) * HALF].unsqueeze(1).broadcast_to([P, heads, HALF])
                ins = dve.tensor_tensor(o2[:, :, z * HALF:(z + 1) * HALF],
                                        q3[:, :, (1 - z) * HALF:(2 - z) * HALF], sin, ALU.mult)
            if g == 0:
                wait(dve, pv_done, after(t - 2, NU, NU))
                ins = dve.tensor_copy(v_t[:, par], src[:, KV:2 * KV])
            ins.then_inc(rope_read, 1)

        def low_q(t, u, half):
            wait(dve, qt_hi, after(t, TURNS, 2 * u + half + 1))
            lo = qt[ROWS:P, u, half * BANK:(half + 1) * BANK]
            dve.tensor_tensor(lo, turn_ps[ROWS:P, :], lo.bitcast(F32), ALU.subtract).then_inc(qt_lo, 1)

        def low_k(t, u):
            wait(dve, kt_hi, after(t, NU, u + 1))
            dve.tensor_tensor(kt[:, u, 1], turn_ps[:], kt[:, u, 0].bitcast(F32), ALU.subtract).then_inc(kt_lo, 1)

        def mask_min(a, c):
            wait(dve, scored, after(a, NC, c + 1))
            wait(dve, expd, after(a, NC, c - 1))
            dve.sem_inc(held)
            for i in range(NI):
                ins = dve.tensor_tensor_reduce(sm[:, c % 2, i * P:(i + 1) * P], s_ps[:, i * P:(i + 1) * P],
                                               mask_t[:], 1.0, 3e38, ALU.add, ALU.min, smin[:, c % 2, i:i + 1])
            ins.then_inc(masked, 1)

        def invert(a, c):
            wait(dve, expd, after(a, NC, c + 1))
            wait(dve, scaled, after(a, NC, c - 1))
            dve.reciprocal(prec[:, c % 2], psum_row[:, c % 2]).then_inc(inverted, 1)

        def read_pt(a, c):
            u, j = divmod(c, NJ)
            wait(dve, p_turned, after(a, NC, c + 1))
            wait(dve, pv_done, after(a - 1, NU, u + 1))
            dve.tensor_copy(pt[:, u, :, j], pt_ps[c % 2][:].rearrange("p (i s) -> p i s", i=NI)).then_inc(pt_read, 1)

        def low_later(n):
            dve.wait_ge(later_hi, n + 1)
            for src, hi, lo in later_parts(n):
                ins = dve.tensor_tensor(lo, src, hi.bitcast(F32), ALU.subtract)
            ins.then_inc(later_lo[0], 1)

        def sum_neighbours(t):
            wait(dve, nb_done, after(t, 2, 2))
            wait(dve, cs_out, after(t, 16, 0))
            dve.tensor_reduce(csum[:, 1], nb[:].rearrange("p (j s) -> p j s", s=S), AX.X, ALU.add).then_inc(summed, 1)

        def invert_norms():
            dve.wait_ge(root, 1)
            dve.tensor_scalar(norm, norm, COS_EPS, None, ALU.max).then_inc(cos_step, 1)
            dve.wait_ge(cos_step, 1)
            dve.reciprocal(norm, norm).then_inc(cos_step, 1)

        def cosine(m):
            value, total = ((own, sqs[:, 0:QD]), (right, nbs))[m]
            if m == 0:
                dve.wait_ge(o_lo, 2)
            dve.wait_ge(cos_step, 2 + m)
            dve.tensor_tensor(value, norm[:, 0:QD], norm[:, m:QD + m], ALU.mult).then_inc(cos_step, 1)
            dve.wait_ge(cos_step, 3 + m)
            dve.tensor_tensor(value, value, total, ALU.mult).then_inc(sim_made, 1)

        for n in range(PIECES):
            dve.wait_ge(w_hi, n + 1)
            dve.tensor_tensor(w_piece(n, 1), stage(n), w_piece(n, 0).bitcast(F32), ALU.subtract).then_inc(w_lo, 1)
            if n == 2 * GP - 1:
                dve.wait_ge(consts_in, 48)
                rotate(0, 0, 0)
            if n == PIECES - 2:
                rotate(0, 0, 1)

        def step(t, par):
            a, b = t - 1, t - 2
            if at_step(t, 0):
                low_k(0, 0)
                dve.wait_ge(x_hi, 2)
                dve.tensor_tensor(xs[:, 1, 1], xraw[:, 1], xs[:, 1, 0].bitcast(F32), ALU.subtract).then_inc(x_lo, 2)
                low_q(0, 0, 0)
                return
            for p in range(NC):
                if p > 0 and valid(a):
                    invert(a, p - 1)
                if p == 0 and valid(b):
                    invert(b, NC - 1)
                if p == 0 and valid(a):
                    low_q(a, 0, 1)
                if p == 7 and valid(t):
                    low_q(t, 0, 0)
                if valid(a):
                    mask_min(a, p)
                if p in (2, 3) and valid(a):
                    low_q(a, 1, p - 2)
                if at_step(t, 1) and p == 0:
                    sum_neighbours(0)
                if p == 3 and valid(t):
                    sum_neighbours(t)
                if p == 4 and valid(t):
                    low_k(t, 0)
                if p < BEHIND and valid(b):
                    read_pt(b, NC - BEHIND + p)
                if p >= BEHIND and valid(a):
                    read_pt(a, p - BEHIND)
                if p == 0 and valid(a):
                    rotate(a, 1 - par, 2)
                if p == 1 and valid(a):
                    low_k(a, 1)
                if p == 2 and valid(t):
                    rotate(t, par, 0)
                if p == 5 and valid(t):
                    rotate(t, par, 1)
                if at_step(t, B - 1) and p in (4, 7):
                    low_later((p - 4) // 3 * 2)
                if at_step(t, B) and p == 0:
                    low_later(3)
                if at_step(t, B) and p == 3:
                    dve.wait_ge(cs_in, 32)
                    edge = sqs[:, QD:QD + 1]
                    dve.tensor_scalar(edge, edge, 0.0, None, ALU.max).then_inc(cs_edge, 1)
                if at_step(t, B) and p in (3, 4, 5):
                    low_later(p + 2)
            if at_step(t, LAST):
                low_later(10)
                invert_norms()
                cosine(0)
                cosine(1)

        steps(dve, step, 0, LAST, LEAD, TAIL)

    @block.scalar
    def _(act):
        def high_x(t, par):
            wait(act, x_in[par], arrivals(t, par))
            wait(act, qkv_done, after(t - 2, NG, NG))
            nc.scalar.copy(xs[:, par, 0], xraw[:, par]).then_inc(x_hi, 1)

        def square(t):
            wait(act, c_in, after(t, 16, 16))
            wait(act, cs_out, after(t, 16, 0))
            for j in range(CB):
                cols = slice(j * S, (j + 1) * S)
                ins = nc.scalar.activation(sq[:, cols], ctx_t[:, cols], ACT.Square, accum_out=csum[:, 0, j:j + 1])
            ins.then_inc(sq_done, 1)

        def high_q(t, u, half):
            wait(act, q_turned, after(t, TURNS, 2 * u + half + 1))
            wait(act, scored, after(t - 1, NC, NJ * (u + 1)))
            nc.scalar.copy(qt[:, u, half * BANK:(half + 1) * BANK], turn_ps[:]).then_inc(qt_hi, 1)

        def high_k(t, u):
            wait(act, kx_turned, after(t, NU, u + 1))
            wait(act, scored, after(t - 1, NC, NJ * (u + 1)))
            nc.scalar.copy(kt[:, u, 0], turn_ps[:]).then_inc(kt_hi, 1)

        def exponent(a, c):
            wait(act, masked, after(a, NC, c + 1))
            wait(act, scaled, after(a, NC, c - 1))
            wait(act, inverted, after(a, NC, c - 1))
            for i in range(NI):
                ins = nc.scalar.activation(pexp[:, c % 2, i * P:(i + 1) * P], sm[:, c % 2, i * P:(i + 1) * P],
                                           ACT.Exp, bias=smin[:, c % 2, i:i + 1], scale=-1.0,
                                           accum_out=psum_row[:, c % 2, i:i + 1])
            ins.then_inc(expd, 1)

        def read_ot(a, u):
            wait(act, pv_done, after(a, NU, u + 1))
            if at_step(a, B - 1) and u == 1:
                act.wait_ge(o_lo, 2)
            else:
                wait(act, ot_out[u], after(a, 16, 0))
            nc.scalar.copy(ot_last if at_step(a, B - 1) and u == 1 else ot[:, u], o_ps[:]).then_inc(ot_read, 1)

        def high_later(n):
            act.wait_ge(qkv_done, after(B - 1, NG, min(n // (KT // 2), 2) + 1))
            parts = later_parts(n)
            arrived = [m for m in range(n + 1) if lands(m) == lands(n)]
            act.wait_ge(later_in[lands(n)], 16 * sum(len(later_parts(m)) for m in arrived))
            for src, hi, _ in parts:
                ins = nc.scalar.copy(hi, src)
            ins.then_inc(later_hi, 1)

        high_x(0, 0)
        for n in range(PIECES):
            act.wait_ge(w_in[n % STAGES], 16 * (n // STAGES + 1))
            nc.scalar.copy(w_piece(n, 0), stage(n)).then_inc(w_hi, 1)

        def take_root():
            act.wait_ge(cs_in, 16 * 2)
            act.wait_ge(cs_edge, 1)
            nc.scalar.activation(norm, sqs, ACT.Sqrt).then_inc(root, 1)

        def high_out(t):
            act.wait_ge(o_in[t], 16)
            act.wait_ge(qkv_done, after(B - 2 + t, NG, NG))
            nc.scalar.copy(halves[:, t, 0].rearrange("p t s -> p (t s)"), raw[:, t]).then_inc(o_hi, 1)

        def step(t, par):
            a, b = t - 1, t - 2
            if at_step(t, 0):
                high_k(0, 0)
                high_x(1, 1)
                square(0)
                high_q(0, 0, 0)
                return
            for p in range(NC):
                if p == 1 and valid(a):
                    high_k(a, 1)
                if p == 0 and valid(a):
                    high_q(a, 0, 1)
                if p in (2, 3) and valid(a):
                    high_q(a, 1, p - 2)
                if p == 2 and valid(t + 1):
                    high_x(t + 1, 1 - par)
                if p == 3 and valid(b):
                    read_ot(b, 1)
                if p == 4 and valid(t):
                    high_k(t, 0)
                if p == 6 and valid(t + 1):
                    square(t + 1)
                if p == 7 and valid(t):
                    high_q(t, 0, 0)
                if p == 7 and valid(a) and not at_step(a, B - 1):
                    read_ot(a, 0)
                if valid(a):
                    exponent(a, p)
                if at_step(t, 1) and p == 1:
                    square(1)
                if at_step(t, B - 1):
                    if p == 2:
                        high_out(0)
                    if p in (3, 4):
                        high_later(p - 3)
                    if p in (6, 7):
                        high_later(p - 4)
                if at_step(t, B):
                    if p == 0:
                        high_later(4)
                    if p in (2, 3, 4, 5):
                        high_later(p + 3)
                    if p == 6:
                        high_out(1)
                    if p == 7:
                        high_later(9)
            if at_step(t, B):
                high_later(10)
                take_root()
                read_ot(B - 1, 0)

        steps(act, step, 0, LAST, LEAD, TAIL)

    @block.gpsimd
    def _(pool):
        def low_x(t, par, half):
            k = slice(half * KT // 2, (half + 1) * KT // 2)
            wait(pool, x_hi, after(t, 1, 1))
            pool.tensor_tensor(xs[:, par, 1, k], xraw[:, par, k], xs[:, par, 0, k].bitcast(F32),
                               ALU.subtract).then_inc(x_lo, 1)

        def neighbour(t, half):
            lo, hi = half * HD, (half + 1) * HD
            wait(pool, c_in, after(t, 16, 16))
            wait(pool, summed, after(t - 1, 1, 1))
            pool.tensor_tensor(nb[:, lo:hi], ctx_t[:, lo:hi], ctx_t[:, lo + S:hi + S], ALU.mult).then_inc(nb_done, 1)

        def add_k(t, par):
            r = par % 2
            wait(pool, rope_read, after(t, NG, 1))
            wait(pool, kx_turned, after(t - 1, NU, NU))
            for u in range(NU):
                cols = slice(u * P, (u + 1) * P)
                one, two = (rot[:, r, cols].rearrange("p (a i d) -> p a i d", a=2, d=DH) for rot in (rot1, rot2))
                for copy in range(2):
                    ins = pool.tensor_tensor(diagonal(kx[:, u].rearrange("p i c -> p (i c)"), copy), one, two, ALU.add)
            ins.then_inc(roped, 1)

        def add_q(t, par, u, half):
            r = (par + 1 + u) % 2
            cols = slice(half * BANK // 2, (half + 1) * BANK // 2)
            wait(pool, rope_read, after(t, NG, 2 + u))
            wait(pool, q_turned, after(t - 1, TURNS, 2 * u + half + 1))
            one, two = (rot[:, r, cols].rearrange("p (n c) -> p n c", c=ROWS).unsqueeze(2)
                        .broadcast_to([P, NJ, 2, ROWS]) for rot in (rot1, rot2))
            pool.tensor_tensor(qn[u][:, half * BANK:(half + 1) * BANK].rearrange("p (n x c) -> p n x c", x=2, c=ROWS),
                               one, two, ALU.add).then_inc(roped, 1)

        def scale(a, c):
            wait(pool, inverted, after(a, NC, c + 1))
            wait(pool, p_turned, after(a, NC, c - 1))
            pool.tensor_tensor(pn[:, c % 2].rearrange("p (i s) -> p i s", i=NI),
                               pexp[:, c % 2].rearrange("p (i s) -> p i s", i=NI),
                               prec[:, c % 2].unsqueeze(2).broadcast_to([P, NI, S]), ALU.mult).then_inc(scaled, 1)

        pool.memset(kx[:], 0.0).then_inc(set_up, 1)
        pool.memset(zero[:], 0.0).then_inc(set_up, 1)
        low_x(0, 0, 0)
        low_x(0, 0, 1)
        pool.wait_ge(set_up, 2)

        def low_later(n):
            pool.wait_ge(later_hi, n + 1)
            for src, hi, lo in later_parts(n):
                ins = pool.tensor_tensor(lo, src, hi.bitcast(F32), ALU.subtract)
            ins.then_inc(later_lo[1], 1)

        def low_out(t, half):
            cols = slice(half * HD, (half + 1) * HD)
            pool.wait_ge(o_hi, t + 1)
            hi, lo = (halves[:, t, part].rearrange("p t s -> p (t s)")[:, cols] for part in range(2))
            pool.tensor_tensor(lo, raw[:, t, cols], hi.bitcast(F32), ALU.subtract).then_inc(o_lo, 1)

        def step(t, par):
            a, b = t - 1, t - 2
            if at_step(t, 0):
                add_k(0, 0)
                add_q(0, 0, 0, 0)
                add_q(0, 0, 0, 1)
                neighbour(0, 0)
                neighbour(0, 1)
                return
            for p in range(NC):
                if p == 3 and valid(t):
                    add_k(t, par)
                if p in (6, 7) and valid(t):
                    add_q(t, par, 0, p - 6)
                if p == 0 and valid(b):
                    scale(b, NC - 1)
                if p == 1 and valid(a):
                    add_q(a, 1 - par, 1, 0)
                if p > 0 and valid(a):
                    scale(a, p - 1)
                if p == 2 and valid(a):
                    add_q(a, 1 - par, 1, 1)
                if p in (2, 3) and valid(t + 1):
                    low_x(t + 1, 1 - par, p - 2)
                if at_step(t, 1) and p == 1:
                    neighbour(1, 0)
                    neighbour(1, 1)
                if p in (5, 7) and valid(t + 1):
                    neighbour(t + 1, (p - 5) // 2)
                if at_step(t, B - 1):
                    if p in (3, 4):
                        low_out(0, p - 3)
                    if p == 6:
                        low_later(1)
                if at_step(t, B) and p in (2, 5):
                    low_later(4 * (p // 3 + 1))
            if at_step(t, LAST):
                low_out(1, 0)
                low_out(1, 1)
                low_later(9)

        steps(pool, step, 0, LAST, LEAD, TAIL)


def sim_row(sim_dram, n, shift):
    row = sim_dram[0, n, 0:1]
    return bass.AP(tensor=row.tensor, offset=row.offset + shift,
                   ap=[[len(SIM_TABLE) * (D + SIM_PAD), B], [D // 4, 4], [1, D // 4]])


def diagonal(blocks, copy):
    return bass.AP(tensor=blocks.tensor, offset=blocks.offset + copy * 2 * DH,
                   ap=[list(blocks.ap[0]), [2 * P, 2], [P + DH, 2], [1, DH]])


def part2(nc, ctx, weights, raw, halves, wo_ps, handoff, x, br, ident, ot_dram, sim_dram, out):
    def sb(name, shape, dt=F32):
        return ctx.enter_context(nc.sbuf_tensor(name, shape, dt))

    def ps(name):
        return ctx.enter_context(nc.psum_tensor(name, [P, BANK], F32))

    def sem(name):
        return ctx.enter_context(nc.semaphore(name))

    wo_sb, wa_sb, wb_sb, wx_sb = later_weights(weights)
    wx_sb = wx_sb.rearrange("p l (k o) -> p l k o", k=TAPS)

    PB = 3
    oraw, os_t = raw, halves
    xn0, xn_in, o_in, o_hi, o_lo, wo_done, ot_out, ot_read, sim_made, sim_out, kept = handoff
    _, right, ot_last = kept
    xn = (xn0, sb("xn1", [P, D]))
    yz = sb("yz", [P, 2, D])
    y3 = sb("y3", [P, D])
    x1 = sb("x1", [P, 2, D + 2])
    att = sb("att", [P, TAPS, D])
    prod = sb("prod", [P, PB, BANK])
    prods = sb("prods", [P, PB, 2, BANK], F32R)
    late = sb("late", [P, 2, 2, D])
    xt = sb("xt", [P, 2, KT, S], F32R)
    br_t = sb("br_t", [P, H])
    id_t = sb("id2_t", [P, P])
    lowhi = sb("lowhi", [P, LOWW])
    low = sb("low", [P, LOWW])
    logit = sb("logit", [P, H])
    nmax = sb("nmax", [P, 1])
    gate = sb("gate", [P, H])
    gsum = sb("gsum", [P, 1])
    grec = sb("grec", [P, 1])
    gated = sb("gated", [P, HR])
    lt = sb("lt", [P, 2, S], F32R)
    power = sb("power", [P, 1])
    stats = [sb(f"stats{n}", [P, 2, 6]) for n in range(3)]
    mv = [sb(f"mv{n}", [P, 2]) for n in range(3)]
    var = [sb(f"var{n}", [P, 1]) for n in range(3)]
    rstd = [sb(f"rstd{n}", [P, 1]) for n in range(3)]
    nmean3 = sb("nmean3", [P, 1])
    shift3 = sb("shift3", [P, 1])

    x2, res = late[:, 0], late[:, 1]
    conv_ps = [ps("conv_ps0"), ps("conv_ps1")]
    ffn_ps = [ps("ffn_ps0"), ps("ffn_ps1")]

    consts_in = sem("consts2_in")
    set_up = sem("set_up2")
    att_in = [sem("att_in0"), sem("att_in1")]
    added = [sem(f"added{n}") for n in range(3)]
    counted = [sem(f"counted{n}") for n in range(3)]
    averaged = [sem(f"averaged{n}") for n in range(3)]
    var_done = [sem(f"var_done{n}") for n in range(3)]
    rstd_done = [sem(f"rstd_done{n}") for n in range(3)]
    normed = [sem(f"normed{n}") for n in range(3)]
    prod_done = sem("prod_done")
    prod_hi = sem("prod_hi")
    prod_lo = sem("prod_lo")
    conv_done = sem("conv_done")
    x2_turned = sem("x2_turned")
    xt_hi = sem("xt_hi")
    xt_lo = sem("xt_lo")
    low_done = sem("low_done")
    low_step = sem("low_step")
    gate_in = sem("gate_in")
    gate_done = sem("gate_done")
    gated_done = sem("gated_done")
    low_turned = sem("low_turned")
    lt_hi = sem("lt_hi")
    lt_lo = sem("lt_lo")
    ffn_done = sem("ffn_done")
    held = sem("held2")
    shifted = sem("shifted")
    stored = [sem("stored0"), sem("stored1")]

    LAST = B + 2
    LEAD, TAIL = 6, 5
    UNITS = 2 * TAPS
    SLOTS2 = 2 * KT
    CONV_AT = (8, 10, 12, 14, 15, 17)
    FIRST_CONV_AT = (11, 13, 15, 17, 18, 20)
    LOWCHAIN = 4

    def ffn_place(t):
        return wo_ps if at_step(t, B - 2) else ffn_ps

    def conv_at(t):
        return FIRST_CONV_AT if at_step(t, 0) else CONV_AT

    block = ctx.enter_context(nc.Block())

    @block.sync
    def _(sp):
        def load_o(t, par):
            wait(sp, o_lo, after(t - 2, 2, 2))
            sp.dma_start(oraw[:, par], ot_dram[t]).then_inc(o_in[par], 16)

        def load_xn(t, par):
            wait(sp, added[0], after(t - 2, 2, 2))
            sp.dma_start(xn[par][:], x[t]).then_inc(xn_in[par], 16)

        def load_att(t, h):
            cols = slice(h * BANK, (h + 1) * BANK)
            wait(sp, prod_done, after(t - 1, UNITS, TAPS * (h + 1)))
            for (first, last), row in zip(RUNS, (0, 2, 3)):
                sp.dma_start(att[first:last, :, cols],
                             sim_dram[t, row, cols].unsqueeze(0).unsqueeze(0).broadcast_to([last - first, TAPS, BANK])
                             ).then_inc(att_in[h], 16)
            rows = sim_dram[t, 0:TAPS, cols]
            both_edges = bass.AP(tensor=rows.tensor, offset=rows.offset, ap=[[2 * (D + SIM_PAD), 2]] + [list(d) for d in rows.ap])
            sp.dma_start(att[EDGES[0]:EDGES[1] + 1:EDGES[1] - EDGES[0], :, cols], both_edges).then_inc(att_in[h], 16)

        sp.wait_ge(sim_made, 2)
        for n, shift in ((0, 1), (1, 1), (3, 0), (4, 0)):
            sp.dma_start(sim_row(sim_dram, n, shift), right).then_inc(sim_out, 16)
        sp.dma_start(id_t[:], ident).then_inc(consts_in, 16)
        sp.dma_start(br_t[:], br).then_inc(consts_in, 16)

        def step(t, par):
            if at_step(t, 0):
                sp.wait_ge(ot_read, NU * B)
                sp.dma_start(ot_dram[B - 1, :, BANK:D], ot_last).then_inc(ot_out[1], 16)
                sp.wait_ge(sim_out, 16 * 7)
                load_att(0, 0)
                load_att(0, 1)
                for u in range(NU):
                    sp.wait_ge(ot_out[u], 16 * B)
            if valid(t + 2):
                load_o(t + 2, par)
            if valid(t + 1):
                load_xn(t + 1, 1 - par)
            if valid(t) and not at_step(t, 0):
                load_att(t, 0)
            if valid(t - 3):
                wait(sp, normed[2], after(t - 3, 1, 1))
                sp.dma_start(out[t - 3], res[:, 1 - par]).then_inc(stored[1 - par], 16)
            if valid(t) and not at_step(t, 0):
                load_att(t, 1)

        steps(sp, step, 0, LAST, LEAD, TAIL)
        for par in range(2):
            sp.wait_ge(stored[par], 16 * B // 2)

    @block.tensor
    def _(pe):
        def project(t, par, n, k):
            if n == 0 and k == 0:
                wait(pe, o_lo, after(t, 2, 2))
            if k == 0:
                wait(pe, added[0], after(t - 1, 2, n + 1))
            for m, (ol, wl) in enumerate(((0, 0), (0, 1), (1, 0))):
                mm = pe.matmul(wo_ps[n][:], os_t[:, par, ol, k], wo_sb[:, wl, k, n * BANK:(n + 1) * BANK],
                               start=(k == 0 and m == 0), stop=(k == KT - 1 and m == 2))
            if k == KT - 1:
                mm.then_inc(wo_done, 1)

        def convolve(t, m):
            h, k = divmod(m, TAPS)
            wait(pe, prod_lo, after(t, UNITS, m + 1))
            if k == 0:
                wait(pe, added[1], after(t - 1, 2, h + 1))
            for n, (wl, xl) in enumerate(((0, 0), (1, 0), (0, 1))):
                mm = pe.matmul(conv_ps[h][:], wx_sb[:, wl, k], prods[:, m % PB, xl],
                               start=(k == 0 and n == 0), stop=(k == TAPS - 1 and n == 2))
            mm.then_inc(conv_done, 1)

        def turn_x2(t, par, n):
            if at_step(t, 0) and n == 0:
                pe.wait_ge(consts_in, 32)
            wait(pe, normed[1], after(t, 1, 1))
            if at_step(t, B - 2):
                pe.wait_ge(added[0], 2 * (B - 1) + n + 1)
            else:
                last = t - 2 if at_step(t, B - 1) else t - 1
                wait(pe, added[2], after(last, 2, n + 1))
            for k in range(NJ):
                c = (n * NJ + k) * P
                mm = pe.transpose(ffn_place(t)[n][:, k * P:(k + 1) * P], x2[:, par, c:c + P], id_t[:])
            mm.then_inc(x2_turned, 1)

        def reduce_rank(t):
            wait(pe, xt_lo, after(t, 2, 2))
            for k in range(KT):
                for xl in range(2):
                    mm = pe.matmul(ffn_place(t)[0][:, 0:2 * LOWW], xt[:, xl, k],
                                   wa_sb[:, k].rearrange("p l n -> p (l n)"),
                                   start=(k == 0 and xl == 0), stop=(k == KT - 1 and xl == 1))
            mm.then_inc(low_done, 1)

        def turn_low(t):
            wait(pe, gated_done, after(t, 1, 1))
            pe.transpose(ffn_place(t)[1][:, 0:S], gated[:], id_t[:]).then_inc(low_turned, 1)

        def expand(t):
            wait(pe, lt_lo, after(t, 1, 1))
            for n in range(2):
                for m, (ll, wl) in enumerate(((0, 0), (0, 1), (1, 0))):
                    mm = pe.matmul(ffn_place(t)[n][:], lt[:, ll], wb_sb[:, wl, n * BANK:(n + 1) * BANK],
                                   start=(m == 0), stop=(m == 2))
                mm.then_inc(ffn_done, 1)

        def step(t, par):
            o, c, f, z = t, t - 1, t - 2, t - 3
            for s in range(SLOTS2):
                if valid(f) and s + SLOTS2 in conv_at(f):
                    convolve(f, conv_at(f).index(s + SLOTS2))
                if valid(c) and s in conv_at(c):
                    convolve(c, conv_at(c).index(s))
                if valid(z) and s == 2:
                    expand(z)
                if valid(f):
                    if s in (9, 10):
                        turn_x2(f, par, s - 9)
                    if s == 13:
                        reduce_rank(f)
                    if s == 15:
                        turn_low(f)
                if valid(o) and not at_step(o, 0):
                    project(o, par, s // KT, s % KT)

        steps(pe, step, 0, B - 1, LEAD, TAIL - 3)

        convolve(B - 2, 5)
        expand(B - 3)
        for m in range(UNITS):
            convolve(B - 1, m)
            if m == 1:
                turn_x2(B - 2, 0, 0)
                turn_x2(B - 2, 0, 1)
        reduce_rank(B - 2)
        turn_x2(B - 1, 1, 0)
        turn_low(B - 2)
        turn_x2(B - 1, 1, 1)
        expand(B - 2)
        reduce_rank(B - 1)
        turn_low(B - 1)
        expand(B - 1)

    @block.vector
    def _(dve):
        dve.memset(power[:], -0.5).then_inc(set_up, 1)
        dve.memset(x1[:, :, 0:1], 0.0).then_inc(set_up, 1)
        dve.memset(x1[:, :, D + 1:D + 2], 0.0).then_inc(set_up, 1)

        def add(t, par, n, half):
            cols = slice(half * BANK, (half + 1) * BANK)
            if n == 0:
                wait(dve, wo_done, after(t, 2, half + 1))
                if half == 0:
                    wait(dve, xn_in[par], arrivals(t, par))
                dst = yz[:, 0, cols]
                ins = dve.tensor_tensor(dst, wo_ps[half][:], xn[par][:, cols], ALU.add)
            elif n == 1:
                wait(dve, conv_done, after(t, UNITS, TAPS * (half + 1)))
                dst = yz[:, 1, cols]
                ins = dve.tensor_tensor(dst, conv_ps[half][:], x1[:, par, 1 + half * BANK:1 + (half + 1) * BANK], ALU.add)
            else:
                wait(dve, ffn_done, after(t, 2, half + 1))
                wait(dve, normed[2], after(t - 1, 1, 1))
                dst = y3[:, cols]
                ins = dve.scalar_tensor_tensor(dst, ffn_place(t)[half][:], FFN_SCALE, x2[:, par, cols], ALU.mult, ALU.add)
            ins.then_inc(added[n], 1)

        def count(t, n, half):
            src = y3 if n == 2 else yz[:, n]
            dve.wait_ge(added[n], after(t, 2, half + 1))
            dve.bn_stats(stats[n][:, half], src[:, half * BANK:(half + 1) * BANK]).then_inc(counted[n], 1)

        def average(t, n):
            dve.wait_ge(counted[n], after(t, 2, 2))
            dve.sem_inc(held)
            dve.bn_aggr(mv[n][:], stats[n][:]).then_inc(averaged[n], 1)
            dve.wait_ge(averaged[n], after(t, 1, 1))
            if n == 2:
                dve.tensor_scalar(nmean3[:], mv[n][:, 0:1], -1.0, None, ALU.mult)
            dve.tensor_scalar(var[n][:], mv[n][:, 1:2], LN_EPS, None, ALU.add).then_inc(var_done[n], 1)

        def normalise(t, par, n):
            src = yz[:, n]
            dst = (x1[:, par, 1:D + 1], x2[:, par])[n]
            wait(dve, rstd_done[n], after(t, 1, 1))
            dve.tensor_scalar(dst, src, mv[n][:, 0:1], rstd[n][:], ALU.subtract, ALU.mult).then_inc(normed[n], 1)

        def multiply(t, par, m):
            h, k = divmod(m, TAPS)
            if k == 0:
                wait(dve, att_in[h], after(t, 64, 64))
            wait(dve, prod_lo, after(t, UNITS, m - PB + 1))
            if m == 0:
                dve.wait_ge(normed[0], after(t, 1, 1))
            dve.tensor_tensor(prod[:, m % PB], att[:, k, h * BANK:(h + 1) * BANK],
                              x1[:, par, h * BANK + k:h * BANK + k + BANK], ALU.mult).then_inc(prod_done, 1)

        def low_x2(t, n):
            wait(dve, xt_hi, after(t, 2, n + 1))
            dst = xt[:, :, n * NJ:(n + 1) * NJ].rearrange("p l t s -> p l (t s)")
            dve.tensor_tensor(dst[:, 1], ffn_place(t)[n][:], dst[:, 0].bitcast(F32), ALU.subtract).then_inc(xt_lo, 1)

        def route(t):
            if at_step(t, 0):
                dve.wait_ge(consts_in, 32)
            wait(dve, low_done, after(t, 1, 1))
            dve.tensor_copy(lowhi[:], ffn_place(t)[0][:, LOWW:2 * LOWW]).then_inc(low_step, 1)
            dve.wait_ge(low_step, after(t, LOWCHAIN, 1))
            dve.tensor_tensor(low[:], ffn_place(t)[0][:, 0:LOWW], lowhi[:], ALU.add).then_inc(low_step, 1)
            dve.wait_ge(low_step, after(t, LOWCHAIN, 2))
            dve.tensor_tensor(logit[:], low[:, HR:LOWW], br_t[:], ALU.add).then_inc(low_step, 1)
            dve.wait_ge(low_step, after(t, LOWCHAIN, 3))
            dve.tensor_reduce(nmax[:], logit[:], AX.X, ALU.max, negate=True).then_inc(gate_in, 1)

        def gate_low(t):
            wait(dve, gate_done, after(t, 1, 1))
            dve.reciprocal(grec[:], gsum[:]).then_inc(low_step, 1)
            dve.wait_ge(low_step, after(t, LOWCHAIN, 4))
            dve.scalar_tensor_tensor(gated[:].rearrange("p (h r) -> p h r", h=H),
                                     low[:, 0:HR].rearrange("p (h r) -> p h r", h=H), grec[:],
                                     gate[:].unsqueeze(2).broadcast_to([P, H, R]),
                                     ALU.mult, ALU.mult).then_inc(gated_done, 1)

        def low_lt(t):
            wait(dve, lt_hi, after(t, 1, 1))
            dve.tensor_tensor(lt[:, 1], ffn_place(t)[1][:, 0:S], lt[:, 0].bitcast(F32), ALU.subtract).then_inc(lt_lo, 1)


        def step(t, par):
            c, f, z = t - 1, t - 2, t - 3
            if valid(c):
                add(c, 1 - par, 0, 1)
                count(c, 0, 1)
                average(c, 0)
            if valid(f):
                add(f, par, 1, 1)
            if valid(c):
                normalise(c, 1 - par, 0)
                multiply(c, 1 - par, 0)
            if valid(f):
                count(f, 1, 1)
            if valid(z):
                add(z, 1 - par, 2, 0)
            if valid(f):
                average(f, 1)
            if valid(z):
                count(z, 2, 0)
            if valid(c):
                multiply(c, 1 - par, 1)
            if valid(f):
                normalise(f, par, 1)
            if valid(z):
                add(z, 1 - par, 2, 1)
                count(z, 2, 1)
            if valid(c):
                multiply(c, 1 - par, 2)
            if valid(f):
                low_x2(f, 0)
            if valid(z):
                average(z, 2)
            if valid(f):
                low_x2(f, 1)
            if valid(t):
                add(t, par, 0, 0)
            if valid(c):
                multiply(c, 1 - par, 3)
            if valid(t):
                count(t, 0, 0)
            if valid(c):
                multiply(c, 1 - par, 4)
                add(c, 1 - par, 1, 0)
            if valid(f):
                route(f)
            if valid(c):
                multiply(c, 1 - par, 5)
            if valid(f):
                gate_low(f)
            if valid(c):
                count(c, 1, 0)
            if valid(f):
                low_lt(f)

        steps(dve, step, 0, B - 1, LEAD, TAIL - 3)

        def finish(t):
            for half in range(2):
                add(t, t % 2, 2, half)
                count(t, 2, half)
            average(t, 2)

        add(B - 1, 1, 0, 1)
        count(B - 1, 0, 1)
        average(B - 1, 0)
        add(B - 2, 0, 1, 1)
        normalise(B - 1, 1, 0)
        for m in range(PB):
            multiply(B - 1, 1, m)
        count(B - 2, 1, 1)
        average(B - 2, 1)
        multiply(B - 1, 1, 3)
        normalise(B - 2, 0, 1)
        multiply(B - 1, 1, 4)
        finish(B - 3)
        low_x2(B - 2, 0)
        multiply(B - 1, 1, 5)
        low_x2(B - 2, 1)
        add(B - 1, 1, 1, 0)
        count(B - 1, 1, 0)
        add(B - 1, 1, 1, 1)
        count(B - 1, 1, 1)
        average(B - 1, 1)
        route(B - 2)
        normalise(B - 1, 1, 1)
        gate_low(B - 2)
        low_x2(B - 1, 0)
        low_lt(B - 2)
        low_x2(B - 1, 1)
        finish(B - 2)
        route(B - 1)
        gate_low(B - 1)
        low_lt(B - 1)
        finish(B - 1)

    @block.scalar
    def _(act):
        def high_o(t, par):
            wait(act, o_in[par], arrivals(t, par))
            wait(act, wo_done, after(t - 2, 2, 2))
            nc.scalar.copy(os_t[:, par, 0].rearrange("p t s -> p (t s)"), oraw[:, par]).then_inc(o_hi, 1)

        def high_prod(t, m):
            wait(act, prod_done, after(t, UNITS, m + 1))
            wait(act, conv_done, after(t, UNITS, m - PB + 1))
            nc.scalar.copy(prods[:, m % PB, 0], prod[:, m % PB]).then_inc(prod_hi, 1)

        def high_x2(t, n):
            wait(act, x2_turned, after(t, 2, n + 1))
            wait(act, low_done, after(t - 1, 1, 1))
            nc.scalar.copy(xt[:, 0, n * NJ:(n + 1) * NJ].rearrange("p t s -> p (t s)"),
                           ffn_place(t)[n][:]).then_inc(xt_hi, 1)

        def gates(t):
            wait(act, gate_in, after(t, 1, 1))
            wait(act, gated_done, after(t - 1, 1, 1))
            nc.scalar.activation(gate[:], logit[:], ACT.Exp, bias=nmax[:], accum_out=gsum[:]).then_inc(gate_done, 1)

        def high_lt(t):
            wait(act, low_turned, after(t, 1, 1))
            wait(act, ffn_done, after(t - 1, 2, 2))
            nc.scalar.copy(lt[:, 0], ffn_place(t)[1][:, 0:S]).then_inc(lt_hi, 1)

        def normalise3(t, par):
            wait(act, shifted, after(t, 1, 1))
            wait(act, stored[par], arrivals(t, par) - 16)
            nc.scalar.activation(res[:, par], y3[:], ACT.Identity, bias=shift3[:], scale=rstd[2][:]).then_inc(normed[2], 1)

        def step(t, par):
            c, f, z = t - 1, t - 2, t - 3
            early = not at_step(t, 0) and not at_step(t, 1)
            if valid(t + 1) and early:
                high_o(t + 1, 1 - par)
            if valid(c):
                high_prod(c, 0)
                high_prod(c, 1)
            if valid(f):
                high_x2(f, 0)
            if valid(c):
                high_prod(c, 2)
            if at_step(t, 1):
                high_o(2, 0)
            if valid(f):
                high_x2(f, 1)
            if valid(c):
                high_prod(c, 3)
            if valid(z):
                normalise3(z, 1 - par)
            if valid(c):
                high_prod(c, 4)
            if valid(f):
                gates(f)
            if valid(c):
                high_prod(c, 5)
            if valid(f):
                high_lt(f)

        steps(act, step, 0, B - 1, LEAD, TAIL - 3)

        for m in range(UNITS):
            high_prod(B - 1, m)
            if m in (3, 4):
                high_x2(B - 2, m - 3)
        normalise3(B - 3, 1)
        gates(B - 2)
        high_x2(B - 1, 0)
        high_lt(B - 2)
        high_x2(B - 1, 1)
        gates(B - 1)
        high_lt(B - 1)
        normalise3(B - 2, 0)
        normalise3(B - 1, 1)

    @block.gpsimd
    def _(pool):
        def low_o(t, par, half):
            cols = slice(half * D // 2, (half + 1) * D // 2)
            wait(pool, o_hi, after(t, 1, 1))
            hi, lo = (os_t[:, par, part].rearrange("p t s -> p (t s)")[:, cols] for part in range(2))
            pool.tensor_tensor(lo, oraw[:, par, cols], hi.bitcast(F32), ALU.subtract).then_inc(o_lo, 1)

        def invert_root(t, n):
            wait(pool, var_done[n], after(t, 1, 1))
            wait(pool, normed[n], after(t - 1, 1, 1))
            pool.tensor_tensor(rstd[n][:], var[n][:], power[:], ALU.pow).then_inc(rstd_done[n], 1)
            if n == 2:
                pool.wait_ge(rstd_done[n], after(t, 1, 1))
                pool.tensor_tensor(shift3[:], nmean3[:], rstd[n][:], ALU.mult).then_inc(shifted, 1)

        def low_prod(t, m):
            wait(pool, prod_hi, after(t, UNITS, m + 1))
            pool.tensor_tensor(prods[:, m % PB, 1], prod[:, m % PB], prods[:, m % PB, 0].bitcast(F32),
                               ALU.subtract).then_inc(prod_lo, 1)

        pool.wait_ge(set_up, 3)

        def step(t, par):
            c, f, z = t - 1, t - 2, t - 3
            if valid(c):
                invert_root(c, 0)
            early = not at_step(t, 0) and not at_step(t, 1)
            if valid(t + 1) and early:
                low_o(t + 1, 1 - par, 0)
            if valid(c):
                low_prod(c, 0)
            if valid(f):
                invert_root(f, 1)
            if valid(c):
                low_prod(c, 1)
            if valid(t + 1) and early:
                low_o(t + 1, 1 - par, 1)
            if valid(c):
                low_prod(c, 2)
            if at_step(t, 1):
                low_o(2, 0, 0)
                low_o(2, 0, 1)
            if valid(z):
                invert_root(z, 2)
            if valid(c):
                for m in range(3, UNITS):
                    low_prod(c, m)

        steps(pool, step, 0, B - 1, LEAD, TAIL - 3)

        invert_root(B - 1, 0)
        for m in range(UNITS):
            low_prod(B - 1, m)
            if m == 0:
                invert_root(B - 2, 1)
        invert_root(B - 3, 2)
        invert_root(B - 1, 1)
        invert_root(B - 2, 2)
        invert_root(B - 1, 2)


def rope_tables():
    inv = np.float32(1.0) / np.float32(10000.0) ** (np.arange(0, DH, 2, dtype=np.float32) / np.float32(DH))
    angle = np.arange(S, dtype=np.float32)[:, None] * inv[None, :].astype(np.float32)
    cos = np.concatenate([np.cos(angle)] * 2, axis=1)
    sin = np.concatenate([-np.sin(angle), np.sin(angle)], axis=1)
    scale = np.array([-float(DH) ** -0.5, 1.0])
    tab = scale[None, :, None, None] * np.stack([cos, sin], axis=1)[:, None]
    return np.ascontiguousarray(tab.astype(np.float32).reshape(S, 2, 2, 1, DH))


def kernel(**inputs):
    import concourse.bacc as bacc
    from concourse.bass_utils import run_bass_kernel_spmd

    f = {k: np.asarray(v) for k, v in inputs.items()}
    heads = (NU, NI, NJ, DH)
    q = f["L0_attn_wq"].reshape(*heads, D).transpose(0, 2, 1, 3, 4).reshape(D, D)
    cols = np.concatenate([f["L0_attn_wk"], f["L0_attn_wv"], q]).reshape(NG, BANK, KT, P)
    low = np.concatenate([f["L0_ffn_A"].reshape(HR, D), f["L0_ffn_Wr"]]).reshape(LOWW, KT, P)
    keys = np.arange(S)
    arrays = {
        "xT": f["x"].reshape(B, S, KT, P).transpose(0, 3, 2, 1),
        "x": f["x"],
        "ctx": np.concatenate([f["ctx_4096"].transpose(0, 2, 1), np.zeros((B, 1, S), np.float32)], axis=1),
        "wqkv": cols.transpose(0, 3, 2, 1),
        "wo": f["L0_attn_wo"].reshape(D, *heads).transpose(2, 4, 1, 3, 0).reshape(P, KT, D),
        "wx": f["L0_xattn_weight"].transpose(1, 2, 0).reshape(S, TAPS * S),
        "wa": low.transpose(2, 1, 0).reshape(P, KT * LOWW),
        "wb": f["L0_ffn_B"].transpose(0, 2, 1).reshape(HR, D),
        "br": np.broadcast_to(f["L0_ffn_br"], (P, H)),
        "rope": rope_tables(),
        "mask": np.where(keys[None, :] > keys[:, None], np.float32(MASKED), np.float32(0.0)),
        "ident": np.eye(P, dtype=np.float32),
    }
    arrays = {f"in_{k}": np.ascontiguousarray(v) for k, v in arrays.items()}
    nc = bacc.Bacc("TRN2", target_bir_lowering=False, num_devices=1)
    args = [nc.dram_tensor(k, v.shape, mybir.dt.from_np(v.dtype), kind="ExternalInput").ap()
            for k, v in arrays.items()]
    out = nc.dram_tensor("out", (B, S, D), F32, kind="ExternalOutput").ap()
    build(nc, *args, out)
    r = run_bass_kernel_spmd(nc, [arrays], core_ids=[0])
    return r.results[0]["out"]
```
